# Optimizing a Trainium2 kernel written in Bass

```python
import numpy as np
import jax
import jax.numpy as jnp

def _softmax(x, axis=-1):
    return jax.nn.softmax(x, axis=axis)

def _gelu(x):
    return jax.nn.gelu(x, approximate=True)

def _silu(x):
    return jax.nn.silu(x)

def _sigmoid(x):
    return jax.nn.sigmoid(x)

def _layernorm(x, axis=-1, eps=1e-05):
    m = jnp.mean(x, axis=axis, keepdims=True)
    v = jnp.var(x, axis=axis, keepdims=True)
    return (x - m) / jnp.sqrt(v + eps)

def _scatter_add(tgt, idx, src, axis=0):
    return tgt.at[idx].add(src)

def _segment_sum(src, seg, n):
    return jax.ops.segment_sum(src, seg, n)
kernel_name = 'mk_vit_tower_d1_tok_img768_r4_5db87c'

def setup_inputs(seed: int=0):
    np.random.seed(seed)
    _w = jnp.asarray

    def _rec_inputs():
        import jax
        import jax.numpy as jnp
        _rk = jax.random.key(seed)
        x = 7.57192e-06 + 1.00007 * jax.random.normal(jax.random.fold_in(_rk, 1), (4, 3, 112, 112), jnp.float32)
        return x
    x = _rec_inputs()

    def _L0_tok_setup():
        import jax, jax.numpy as jnp
        import numpy as np
        QMAX = 127.0

        def fake_quant(v):
            s = jnp.maximum(jnp.max(jnp.abs(v)), 1e-08) / QMAX
            return jnp.round(jnp.clip(v / s, -QMAX, QMAX)) * s
        key = jax.random.key(seed)
        k1, k2, k3 = jax.random.split(key, 3)
        B, C, H, W = (64, 3, 224, 224)
        D, P = (192, 8)
        x = jax.random.normal(k1, (B, C, H, W), dtype=jnp.float32)
        w = jax.random.normal(k2, (D, C, P, P), dtype=jnp.float32) * 0.02
        b = jax.random.normal(k3, (D,), dtype=jnp.float32) * 0.02
        return {'x': x, 'w': w, 'b': b}
    _L0_tok_all = _L0_tok_setup()
    _L0_tok_in = {k: v for k, v in _L0_tok_all.items() if k in ('w', 'b')}
    del _L0_tok_all

    def _L0_attn_setup():
        import jax, jax.numpy as jnp
        import numpy as np
        B, N, E, H = (8, 256, 192, 12)
        HD = E // H
        key = jax.random.key(seed)
        k1, k2, k3, k4, k5 = jax.random.split(key, 5)
        s = 0.02
        return {'query': jax.random.normal(k1, (B, N, E), dtype=jnp.float32), 'qkv_w': jax.random.normal(k2, (3 * E, E), dtype=jnp.float32) * s, 'qkv_b': jax.random.normal(k3, (3 * E,), dtype=jnp.float32) * s, 'out_w': jax.random.normal(k4, (E, E), dtype=jnp.float32) * s, 'out_b': jax.random.normal(k5, (E,), dtype=jnp.float32) * s}
    _L0_attn_all = _L0_attn_setup()
    _L0_attn_in = {k: v for k, v in _L0_attn_all.items() if k in ('qkv_w', 'qkv_b', 'out_w', 'out_b')}
    del _L0_attn_all

    def _L0_ffn_setup():
        import jax, jax.numpy as jnp
        import numpy as np
        D_MODEL = 192
        N_EXPERTS = 16
        TOP_K = 2
        D_FF = 4 * D_MODEL
        B, L = (4, 512)
        key = jax.random.key(seed)
        ks = jax.random.split(key, 6)
        s_in = 1.0 / np.sqrt(D_MODEL)
        s_ff = 1.0 / np.sqrt(D_FF)
        x = jax.random.normal(ks[0], (B, L, D_MODEL), dtype=jnp.float32)
        Wr = jax.random.uniform(ks[1], (N_EXPERTS, D_MODEL), jnp.float32, -s_in, s_in)
        W1 = jax.random.uniform(ks[2], (N_EXPERTS, D_MODEL, D_FF), jnp.float32, -s_in, s_in)
        b1 = jax.random.uniform(ks[3], (N_EXPERTS, D_FF), jnp.float32, -s_in, s_in)
        W2 = jax.random.uniform(ks[4], (N_EXPERTS, D_FF, D_MODEL), jnp.float32, -s_ff, s_ff)
        b2 = jax.random.uniform(ks[5], (N_EXPERTS, D_MODEL), jnp.float32, -s_ff, s_ff)
        return {'x': x, 'Wr': Wr, 'W1': W1, 'b1': b1, 'W2': W2, 'b2': b2}
    _L0_ffn_all = _L0_ffn_setup()
    _L0_ffn_in = {k: v for k, v in _L0_ffn_all.items() if k in ('Wr', 'W1', 'b1', 'W2', 'b2')}
    del _L0_ffn_all
    return {'x': x, 'L0_tok_w': _L0_tok_in['w'], 'L0_tok_b': _L0_tok_in['b'], 'L0_attn_qkv_w': _L0_attn_in['qkv_w'], 'L0_attn_qkv_b': _L0_attn_in['qkv_b'], 'L0_attn_out_w': _L0_attn_in['out_w'], 'L0_attn_out_b': _L0_attn_in['out_b'], 'L0_ffn_Wr': _L0_ffn_in['Wr'], 'L0_ffn_W1': _L0_ffn_in['W1'], 'L0_ffn_b1': _L0_ffn_in['b1'], 'L0_ffn_W2': _L0_ffn_in['W2'], 'L0_ffn_b2': _L0_ffn_in['b2']}

def reference(x, L0_tok_w, L0_tok_b, L0_attn_qkv_w, L0_attn_qkv_b, L0_attn_out_w, L0_attn_out_b, L0_ffn_Wr, L0_ffn_W1, L0_ffn_b1, L0_ffn_W2, L0_ffn_b2):
    import jax
    import jax.numpy as jnp

    def _L0_tok_ref(x, w, b):
        import jax, jax.numpy as jnp
        import numpy as np
        QMAX = 127.0

        def fake_quant(v):
            s = jnp.maximum(jnp.max(jnp.abs(v)), 1e-08) / QMAX
            return jnp.round(jnp.clip(v / s, -QMAX, QMAX)) * s
        B, C, H, W = x.shape
        D, _, P, _ = w.shape
        gh, gw = (H // P, W // P)
        xq = fake_quant(x)
        wq = fake_quant(w)
        xp = xq.reshape(B, C, gh, P, gw, P)
        out = jnp.einsum('bchpwq,dchq->bhwd', xp.transpose(0, 1, 2, 3, 4, 5), wq, optimize=True) if False else jnp.einsum('bcxpyq,dcpq->bxyd', xp, wq)
        out = out + b
        out = out.reshape(B, gh * gw, D)
        return out

    def _L0_attn_ref(query, qkv_w, qkv_b, out_w, out_b):
        import jax, jax.numpy as jnp
        import numpy as np
        B, N, E, H = (8, 256, 192, 12)
        HD = E // H
        b, n, e = query.shape
        scale = HD ** (-0.5)
        qkv = query @ qkv_w.T + qkv_b
        qkv = qkv.reshape(b, n, 3, H, HD)
        q = qkv[:, :, 0].transpose(0, 2, 1, 3)
        k = qkv[:, :, 1].transpose(0, 2, 1, 3)
        v = qkv[:, :, 2].transpose(0, 2, 1, 3)
        attn = jnp.einsum('bhqd,bhkd->bhqk', q, k) * scale
        attn = jax.nn.softmax(attn, axis=-1)
        x = jnp.einsum('bhqk,bhkd->bhqd', attn, v)
        x = x.transpose(0, 2, 1, 3).reshape(b, n, e)
        return x @ out_w.T + out_b

    def _L0_ffn_ref(x, Wr, W1, b1, W2, b2):
        import jax, jax.numpy as jnp
        import numpy as np
        D_MODEL = 192
        N_EXPERTS = 16
        TOP_K = 2
        D_FF = 4 * D_MODEL
        B, L = (4, 512)
        logits = jnp.einsum('bld,ed->ble', x, Wr)
        probs = jax.nn.softmax(logits, axis=-1)
        top_p, top_idx = jax.lax.top_k(probs, TOP_K)
        gating = jnp.sum(jax.nn.one_hot(top_idx, N_EXPERTS, dtype=probs.dtype) * top_p[..., None], axis=-2)
        gate_e = jnp.moveaxis(gating, -1, 0)

        def step(y, params):
            W1e, b1e, W2e, b2e, ge = params
            h = jax.nn.gelu(jnp.einsum('bld,df->blf', x, W1e) + b1e, approximate=False)
            out = jnp.einsum('blf,fd->bld', h, W2e) + b2e
            return (y + ge[..., None] * out, None)
        y0 = jnp.zeros_like(x)
        y, _ = jax.lax.scan(step, y0, (W1, b1, W2, b2, gate_e))
        return x + y
    h = _L0_tok_ref(x, L0_tok_w, L0_tok_b)
    h = h + _L0_attn_ref(_layernorm(h, axis=-1), L0_attn_qkv_w, L0_attn_qkv_b, L0_attn_out_w, L0_attn_out_b)
    h = h + _L0_ffn_ref(_layernorm(h, axis=-1), L0_ffn_Wr, L0_ffn_W1, L0_ffn_b1, L0_ffn_W2, L0_ffn_b2)
    return h

_drawn_inputs = setup_inputs


def setup_inputs(seed=0):
    import zlib

    import numpy as np

    out = dict(_drawn_inputs(seed))
    spreads = {}
    factors = {'L0_attn_qkv_b': 2.925, 'L0_ffn_b1': 25.421, 'L0_ffn_b2': 8.0}
    for name, (base, spread) in spreads.items():
        noise = np.random.default_rng([zlib.crc32(name.encode()), seed]).standard_normal(out[name].shape)
        drawn = base * np.exp(spread * noise) if base else spread * noise
        out[name] = jnp.asarray(drawn.astype(out[name].dtype))
    for name, factor in factors.items():
        out[name] = (out[name] * factor).astype(out[name].dtype)
    return out
```

```python
from contextlib import ExitStack

import concourse.bass as bass
from concourse import mybir

F32 = mybir.dt.float32
BF16 = mybir.dt.bfloat16
U32 = mybir.dt.uint32
I32 = mybir.dt.int32
ALU = mybir.AluOpType
ACT = mybir.ActivationFunctionType
AX = mybir.AxisListType.X

P = 128
IMG = 4
TP = 98
NQ = 2 * TP
NT = 2 * IMG
TOK = NT * TP
D = 192
KC = 96
H, HD = 12, 16
G6 = 6
KA = KC + H
NE, FF = 16, 768
FC = FF // P
CAP = P
NOV = 12
ROW = D + 2
RING = 8
W2R = FC * D + FC
LAG = 2
MAGIC = 12582912.0
BIG = 65536.0
EPS = 1e-5

C_ID, C_HM, C_REV, C_E128, C_THR, C_TRI16, C_OVC, C_I12, C_LT = 0, 128, 140, 156, 172, 178, 434, 450, 462
C_N = C_LT + TP


def schedule():
    order = [("A1", 0, 0), ("A2q", 0, 0), ("A2k", 0, 0), ("A3", 0, 0), ("KB", 0, 0)]
    for b in range(-1, IMG + 1):
        for s in range(H):
            if 0 <= b < IMG:
                order.append(("C", b, s))
            if b + 1 < IMG:
                chunks = (2 * s, 2 * s + 1) if s < 2 else (s + 2,) if s < 10 else ()
                order += [("B", b + 1, i) for i in chunks]
            at = {0: [("E2", b - 2)], 2: [("LN", b + 2)], 3: [("D1", b - 1), ("A1", b + 2)], 4: [("E3", b - 2)],
                  5: [("D2", b - 1), ("A2q", b + 2)], 6: [("A2k", b + 2), ("D3", b - 1)], 8: [("A3", b + 2)],
                  9: [("KB", b + 2)], 11: [("N", b + 1), ("E1", b - 1)]}.get(s, [])
            for kind, c in at:
                if 0 <= c < IMG:
                    order.append((kind, c, 0))
    order += [("E2", IMG - 1, 0), ("E3", IMG - 1, 0)]
    return order


def vit_block(nc, xp, wtok, tokb, wqkv, qkb, vb, wout, outb, wr, w1, w2, b2, consts, own, out):
    order = schedule()
    pieces = []
    for kind, b, _ in order:
        if kind == "D1":
            pieces += [("D1", b, 0), ("D1", b, 1)]
        elif kind not in ("B", "C", "LN", "KB"):
            pieces.append((kind, b, 0))
    piece = {p: n for n, p in enumerate(pieces)}

    with ExitStack() as ctx:
        def sb(name, shape, dt=F32):
            return ctx.enter_context(nc.sbuf_tensor(name, shape, dt))

        def sem(name):
            return ctx.enter_context(nc.semaphore(name))

        ps = ctx.enter_context(nc.psum_tensor("ps", [P, 8, 512], F32))
        slots = nc.dram_tensor("slots", ((NE + NOV) * CAP, ROW), F32, kind="Internal").ap()

        con = sb("con", [P, C_N])
        x_sb = sb("x_sb", [TP, 2 * TOK])
        warm = sb("warm", [P, 2])
        xq = sb("xq", [KC, 2, TOK], BF16)
        wt_sb = sb("wt_sb", [KC, 2 * D])
        wtq = sb("wtq", [KC, 2, D], BF16)
        amax = sb("amax", [KC, 2])
        qs = sb("qs", [2, 4])
        sc = sb("sc", [P, 5])
        ones = sb("ones", [P, P])
        onesb = sb("onesb", [TP, TP], BF16)
        ltb = sb("ltb", [TP, TP], BF16)
        wqkv_sb = sb("wqkv_sb", [KC, 2, 3 * D])
        wo_sb = sb("wo_sb", [KC, 2, D])
        wr_sb = sb("wr_sb", [KC, 2, NE])
        qkb_sb = sb("qkb_sb", [KC, 4])
        rowb = sb("rowb", [TP, 3, D])
        h = sb("h", [TP, NT, D])
        stats = sb("stats", [TP, NT, 6])
        mv = sb("mv", [TP, NT, 2])
        rstd = sb("rstd", [TP, NT])
        nw = sb("nw", [TP, 2, 2])
        xn1 = sb("xn1", [TP, NT, D])
        xnT = sb("xnT", [KC, 2, NQ])
        qaug = sb("qaug", [KA, 3, 2, NQ])
        qbf = sb("qbf", [KC, 2, 2, NQ], BF16)
        ksb = sb("ksb", [KC, 2, NQ])
        room = sb("room", [P, 3 * H * NQ])
        kmask = room[0:KA, :].rearrange("p (b h n) -> p b h n", b=3, h=H)
        kmb = sb("kmb", [KC, 2, H, NQ], BF16)
        vaug = sb("vaug", [TP, 3, 2, H, 32])
        mx = sb("mx", [TP, 2, P])
        prob = x_sb[:, 0:4 * 2 * NQ].rearrange("p (b k n) -> p b k n", b=4, k=2)
        oT = sb("oT", [P, 2, 3, NQ])
        rec = sb("rec", [TP, 2, H])
        otok = sb("otok", [TP, 2, D])
        oTT = sb("oTT", [KC, 2, NQ])
        rows = [sb(f"rows{k}", [TP, NT, ROW]) for k in range(2)]
        base = xn1
        xn2T = sb("xn2T", [KC, 2, NQ])
        lg = sb("lg", [TP, 2, NE])
        lmax = sb("lmax", [TP, 8, 2])
        pr = sb("pr", [TP, 6, 2, NE])
        oh = sb("oh", [TP, 2, NT, NE])
        maskb = sb("maskb", [TP, 2, NE], BF16)
        acc = sb("acc", [TP, IMG + 1, NE], BF16)
        rkv = sb("rkv", [TP, NT, NE])
        big = sb("big", [TP, 2, NE])
        sel = sb("sel", [TP, 2, 2, NE])
        slotf = sb("slotf", [TP, IMG, 2, 2])
        slotu = sb("slotu", [TP, IMG, 2, 2], U32)
        tokid = sb("tokid", [TP, NT], U32)
        padrow = sb("padrow", [P, ROW])
        ring1 = sb("ring1", [KC, RING, 2 * FF])
        ring2 = sb("ring2", [P, RING, W2R])
        ringb = sb("ringb", [P, RING, D])
        taken = [0]

        def view(width):
            taken[0] += width
            return room[:, taken[0] - width:taken[0]]

        xs = view(NE * ROW).rearrange("p (e c) -> p e c", e=NE)
        xsT = view(4 * CAP)[0:KC, :].rearrange("p (b k n) -> p b k n", b=2, k=2)
        hT = view(FC * CAP).rearrange("p (m n) -> p m n", m=FC)
        eo = view(2 * D).rearrange("p (b d) -> p b d", b=2)
        eog = view(2 * D).rearrange("p (b d) -> p b d", b=2)
        extra_cmp = view(NE * NE)[0:TP, :]
        extra_e = view(3 * NE)[0:TP, :].rearrange("p (i e) -> p i e", i=3)
        extra_val = view(2 * NT * NE)[0:TP, :].rearrange("p (i t e) -> p i t e", i=2, t=NT)
        extra_sel = view(2 * NT * NE)[0:TP, :].rearrange("p (k t e) -> p k t e", k=2, t=NT)
        extra_slotf = view(2 * NT)[0:TP, :].rearrange("p (k t) -> p k t", k=2)
        extra_slot = view(2 * NT)[0:TP, :].bitcast(U32).rearrange("p (k t) -> p k t", k=2)
        extra_idf = view(NOV + 1)[0:1, :]
        extra_id = view(NOV + 1)[0:1, :].bitcast(I32)

        ident = con[:, C_ID:C_ID + P]

        con_in, x_in, wt_in, small_in, row_in, pad_in = (sem(n) for n in
            ("con_in", "x_in", "wt_in", "small_in", "row_in", "pad_in"))
        ring_in = [sem(f"ring_in{i}") for i in range(RING)]
        own_in, scales_ready, quantised_pool = sem("own_in"), sem("scales_ready"), sem("quantised_pool")
        dve_link, pool_link = sem("dve_link"), sem("pool_link")
        pool_set = sem("pool_set")
        amax_ready, amax_turned, scale_diag, scale_spread, quantised = (sem(n) for n in
            ("amax_ready", "amax_turned", "scale_diag", "scale_spread", "quantised"))
        tok_done, h_ready, xn1_ready = sem("tok_done"), sem("h_ready"), sem("xn1_ready")
        misc_ready = sem("misc_ready")
        bank_read = [sem(f"bank_read{i}") for i in range(2)]
        kmask_ready, kmb_ready, hb_ready = sem("kmask_ready"), sem("kmb_ready"), sem("hb_ready")
        s_done, mx_ready = sem("s_done"), sem("mx_ready")
        st_done, exp_done, pv_done, oT_ready = (sem(n) for n in ("st_done", "exp_done", "pv_done", "oT_ready"))
        xn2_ready, lexp_ready, mask_ready, slot_ready, base_ready, rows_ready = (sem(n) for n in
            ("xn2_ready", "lexp_ready", "mask_ready", "slot_ready", "base_ready", "rows_ready"))
        base_out, scattered = sem("base_out"), sem("scattered")
        xs_in = [sem(f"xs_in{i}") for i in range(4)]
        t_done, xsT_ready, w1_done, gelu_done, w2_done, eo_ready, eog_ready = (sem(n) for n in
            ("t_done", "xsT_ready", "w1_done", "gelu_done", "w2_done", "eo_ready", "eog_ready"))
        added = sem("added")
        acc_ready, counted, counts_read, extra_known, extra_scattered = (sem(n) for n in
            ("acc_ready", "counted", "counts_read", "extra_known", "extra_scattered"))
        extra_seen = sem("extra_seen")
        extra_in, extra_turned, extra_x, extra_w1, extra_gelu, extra_w2, extra_sum, extra_out, extra_added = (
            sem(n) for n in ("extra_in", "extra_turned", "extra_x", "extra_w1", "extra_gelu", "extra_w2",
                             "extra_sum", "extra_out", "extra_added"))

        out_rows = out[0:TOK, :]
        block = ctx.enter_context(nc.Block())

        def bank_of(kind, b, i=0):
            return 6 + piece[(kind, b, i)] % 2

        def bank_is_free(pe, kind, b, i=0):
            n = piece[(kind, b, i)]
            if n >= 2:
                pe.wait_ge(bank_read[n % 2], n // 2)

        def computed(eng, kind, b, i=0):
            eng.wait_ge(misc_ready, piece[(kind, b, i)] + 1)

        def read_out(eng, kind, b, i=0):
            n = piece[(kind, b, i)]
            eng.wait_ge(bank_read[n % 2], n // 2 + 1)

        def freed_by(kind, b, i=0):
            return bank_read[piece[(kind, b, i)] % 2]

        def extra_tiles(eng):
            eng.wait_ge(extra_known, 1)
            return eng.value_load(extra_id[0:1, NOV:NOV + 1], min_val=0, max_val=NOV)

        def later_tiles(eng, n, tile):
            with eng.If(n > 1):
                with eng.Fori(1, NOV) as i:
                    with eng.If(i < n):
                        tile(i)

        @block.sync
        def _(sp):
            sp.dma_start(x_sb[0:KC, :], xp).then_inc(x_in, 16)
            sp.dma_start(wt_sb[:, :], wtok).then_inc(wt_in, 16)
            sp.dma_start(wqkv_sb[:, :, :], wqkv).then_inc(small_in, 16)
            sp.dma_start(wo_sb[:, :, :], wout).then_inc(small_in, 16)
            sp.dma_start(wr_sb[:, :, :], wr).then_inc(small_in, 16)

            def load_expert(e):
                r = e % RING
                sp.dma_start(ring1[:, r, :], w1[e]).then_inc(ring_in[r], 16)
                sp.dma_start(ring2[:, r, :], w2[e]).then_inc(ring_in[r], 16)
                sp.dma_start(ringb[:, r, :], b2[e:e + 1, :].to_broadcast([P, D])).then_inc(ring_in[r], 16)

            for e in range(RING):
                load_expert(e)
            for b in range(IMG):
                sp.wait_ge(base_ready, b + 1)
                sp.dma_start(out_rows[NQ * b:NQ * (b + 1), :].rearrange("(t p) d -> p t d", p=TP),
                             base[:, 2 * b:2 * b + 2, :]).then_inc(base_out, 16)
            sp.wait_ge(scattered, 16 * 2 * NT)
            for i in range(4):
                sp.dma_start(xs[:, 4 * i:4 * i + 4, :],
                             slots[4 * i * CAP:4 * (i + 1) * CAP, :].rearrange("(e p) c -> p e c", p=CAP)
                             ).then_inc(xs_in[i], 16)
            for e in range(RING, NE):
                sp.wait_ge(eo_ready, e - RING + 1)
                load_expert(e)

            def load_extra(i):
                e = sp.value_load(extra_id[0:1, bass.ds(i, 1)], min_val=0, max_val=NE - 1)
                sp.dma_start(ring1[:, 0, :], w1[bass.ds(e, 1), :, :].rearrange("e p f -> (e p) f")
                             ).then_inc(extra_in, 16)
                sp.dma_start(ring2[:, 0, :], w2[bass.ds(e, 1), :, :].rearrange("e p f -> (e p) f")
                             ).then_inc(extra_in, 16)
                sp.dma_start(ringb[:, 0, :], b2[bass.ds(e, 1), :].to_broadcast([P, D])).then_inc(extra_in, 16)
                sp.dma_start(xs[:, 0, :], slots[bass.ds(i * CAP + NE * CAP, CAP), :]).then_inc(extra_in, 16)

            n = extra_tiles(sp)
            with sp.If(n > 0):
                sp.wait_ge(eo_ready, RING + 1)
                sp.wait_ge(added, 16)
                sp.wait_ge(extra_scattered, 16 * 2 * NT)
                load_extra(0)

            def extra_tile(i):
                sp.wait_ge(extra_added, 16 * i)
                load_extra(i)

            later_tiles(sp, n, extra_tile)

        def image(ap, b):
            return ap.rearrange("p (k n) -> p k n", k=2)[:, :, NQ * b:NQ * (b + 1)]

        def quantise(engine, src, dst, s, link, done):
            link(engine.tensor_scalar(src, src, sc[0:KC, 3 + s:4 + s], 127.0, ALU.mult, ALU.min))
            link(engine.tensor_scalar(src, src, -127.0, MAGIC, ALU.max, ALU.add))
            engine.tensor_scalar(dst, src, MAGIC, None, ALU.subtract).then_inc(done, 1)

        @block.gpsimd
        def _(pool):
            nc.gpsimd.iota(tokid[:, :], pattern=[[TP, NT]], base=0, channel_multiplier=1).then_inc(pool_link, 1)
            nc.gpsimd.memset(padrow[:, 0:ROW - 1], 0.0).then_inc(pool_link, 1)
            nc.gpsimd.iota(padrow[:, ROW - 1:ROW].bitcast(U32), pattern=[[0, 1]], base=TOK,
                           channel_multiplier=1).then_inc(pool_set, 1)
            pool.wait_ge(pool_link, 1)
            for k in range(2):
                nc.gpsimd.tensor_copy(rows[k][:, :, ROW - 1:ROW].bitcast(U32),
                                      tokid[:, :].unsqueeze(2)).then_inc(pool_set, 1)
            nc.gpsimd.memset(vaug[:, :, :, :, HD:32], 1.0).then_inc(pool_set, 1)
            nc.gpsimd.memset(mx[:, :, 0:KC], 0.0).then_inc(pool_set, 1)
            pool.wait_ge(con_in, 16)
            pool_links = [2]

            def link(ins):
                pool_links[0] += 1
                ins.then_inc(pool_link, 1)
                pool.wait_ge(pool_link, pool_links[0])

            pool.wait_ge(scales_ready, 1)
            for b in (2, 3):
                quantise(nc.gpsimd, image(x_sb[0:KC, :], b), xq[:, :, NQ * b:NQ * (b + 1)], 0, link, quantised_pool)
            pool.wait_ge(row_in, 64)
            for kind, b, _ in order:
                if kind == "A1":
                    pool.wait_ge(xn1_ready, 2 * (b + 1))
                    nc.gpsimd.tensor_tensor(h[:, 2 * b:2 * b + 2, :], h[:, 2 * b:2 * b + 2, :],
                                            rowb[:, 2, :].unsqueeze(1).to_broadcast([TP, 2, D]),
                                            ALU.add).then_inc(hb_ready, 1)
                if kind == "A2k":
                    read_out(pool, "A2k", b)
                    if b >= 3:
                        pool.wait_ge(st_done, H * (b - 2))
                    for g in range(2):
                        nc.gpsimd.tensor_tensor(
                            kmask[0:KC, b % 3, G6 * g:G6 * (g + 1), :],
                            ksb[:, g, :].unsqueeze(1).to_broadcast([KC, G6, NQ]),
                            con[0:KC, C_HM:C_HM + G6].unsqueeze(2).to_broadcast([KC, G6, NQ]),
                            ALU.mult).then_inc(kmask_ready, 1)
                if kind == "E1":
                    pool.wait_ge(xn2_ready, 2 * (b + 1))
                    nc.gpsimd.tensor_copy(rows[1][:, 2 * b:2 * b + 2, 0:D],
                                          rows[0][:, 2 * b:2 * b + 2, 0:D]).then_inc(rows_ready, 1)
                    nc.gpsimd.tensor_tensor(base[:, 2 * b:2 * b + 2, :], h[:, 2 * b:2 * b + 2, :],
                                            rows[0][:, 2 * b:2 * b + 2, 0:D], ALU.add).then_inc(base_ready, 1)
                if kind == "E3":
                    if b == 0:
                        pool.wait_ge(pad_in, 32)
                        pool.wait_ge(pool_set, 3)
                    pool.wait_ge(rows_ready, b + 1)
                    pool.wait_ge(slot_ready, b + 1)
                    for i in range(2):
                        for k in range(2):
                            nc.gpsimd.indirect_dma_start(
                                slots, bass.IndirectOffsetOnAxis(slotu[:, b, k, i:i + 1], axis=0),
                                rows[k][:, 2 * b + i, :], None,
                                bounds_check=NE * CAP - 1, oob_is_err=False).then_inc(scattered, 16)
            pool.wait_ge(base_out, 16 * IMG)
            for e in range(NE):
                pool.wait_ge(eog_ready, e + 1)
                if e:
                    pool.wait_ge(added, 16 * e)
                nc.gpsimd.indirect_dma_start(
                    out, bass.IndirectOffsetOnAxis(xs[:, e, ROW - 1:ROW].bitcast(U32), axis=0),
                    eog[:, e % 2, :], None, compute_op=ALU.add).then_inc(added, 16)
                if e == 0:
                    n = extra_tiles(pool)
                if e < NT:
                    with pool.If(n > 0):
                        for k in range(2):
                            nc.gpsimd.indirect_dma_start(
                                slots, bass.IndirectOffsetOnAxis(extra_slot[:, k, e:e + 1], axis=0),
                                rows[k][:, e, :], None,
                                bounds_check=(NE + NOV) * CAP - 1, oob_is_err=False).then_inc(extra_scattered, 16)
            pool.wait_ge(added, 16 * NE)

            def extra_tile(i):
                pool.wait_ge(extra_out, i + 1)
                pool.sem_inc(extra_seen, 1)
                nc.gpsimd.indirect_dma_start(
                    out, bass.IndirectOffsetOnAxis(xs[:, 0, ROW - 1:ROW].bitcast(U32), axis=0),
                    eog[:, 0, :], None, compute_op=ALU.add).then_inc(extra_added, 16)
                pool.wait_ge(extra_added, 16 * i + 16)

            with pool.If(n > 0):
                extra_tile(0)
            later_tiles(pool, n, extra_tile)

        def bring_group(act, group):
            act.wait_ge(pv_done, 4 * group + 4)
            b = group // 3
            if b >= 2:
                computed(act, "D1", b - 2, 1)
            nc.scalar.copy(oT[:, b % 2, group % 3, :],
                           ps[:, 4 + group % 2, 0:NQ]).then_inc(oT_ready, 1)

        @block.scalar
        def _(act):
            act.dma_start(con[:, :], consts).then_inc(con_in, 16)
            act.wait_ge(pool_link, 2)
            nc.scalar.activation(warm[:, 0:1], padrow[:, 0:1], ACT.Exp)
            act.dma_start(rowb[:, 0, :], tokb.to_broadcast([TP, D])).then_inc(row_in, 16)
            act.dma_start(qkb_sb[:, :], qkb).then_inc(row_in, 16)
            act.dma_start(rowb[:, 1, :], vb.to_broadcast([TP, D])).then_inc(row_in, 16)
            act.dma_start(rowb[:, 2, :], outb.to_broadcast([TP, D])).then_inc(row_in, 16)
            act.wait_ge(pool_link, 2)
            act.wait_ge(pool_set, 1)
            act.dma_start(slots.rearrange("(t p) c -> p t c", p=CAP),
                          padrow[:, :].unsqueeze(1).to_broadcast([P, NE + NOV, ROW])).then_inc(pad_in, 16)
            act.dma_start(out[TOK:TOK + P, :], padrow[:, 0:D]).then_inc(pad_in, 16)

            for i in range(3):
                act.dma_start(kmask[KC:KA, i, :, :], own).then_inc(own_in, 16)

            act.wait_ge(row_in, 64)
            for kind, b, s in order:
                if kind in ("A1", "A2q", "A2k", "D2", "E1"):
                    pb = ps[0:KC, bank_of(kind, b), 0:2 * NQ].rearrange("p (k n) -> p k n", k=2)
                    computed(act, kind, b)
                if kind == "A1":
                    if b:
                        computed(act, "A3", b - 1)
                    nc.scalar.copy(xnT[:, :, :], pb).then_inc(freed_by(kind, b), 1)
                if kind == "A2q":
                    if b >= 3:
                        act.wait_ge(st_done, H * (b - 2))
                    if b >= 2:
                        act.wait_ge(s_done, H * (b - 1))
                    for g in range(2):
                        nc.scalar.activation(qbf[:, b % 2, g, :], pb[:, g, :], ACT.Identity,
                                             bias=qkb_sb[:, g:g + 1])
                        last = nc.scalar.activation(qaug[0:KC, b % 3, g, :], pb[:, g, :], ACT.Identity,
                                                    bias=qkb_sb[:, g:g + 1])
                    last.then_inc(freed_by(kind, b), 1)
                if kind == "A2k":
                    if b:
                        act.wait_ge(kmask_ready, 2 * b)
                    for g in range(2):
                        last = nc.scalar.activation(ksb[:, g, :], pb[:, g, :], ACT.Identity,
                                                    bias=qkb_sb[:, 2 + g:3 + g])
                    last.then_inc(freed_by(kind, b), 1)
                if kind == "KB":
                    if b >= 2:
                        act.wait_ge(s_done, H * (b - 1))
                    for g in range(2):
                        act.wait_ge(kmask_ready, 2 * b + g + 1)
                        nc.scalar.copy(kmb[:, b % 2, G6 * g:G6 * (g + 1), :],
                                       kmask[0:KC, b % 3, G6 * g:G6 * (g + 1), :]).then_inc(kmb_ready, 1)
                if kind == "C":
                    n = H * b + s
                    act.wait_ge(st_done, n + 1)
                    if n >= 4:
                        act.wait_ge(pv_done, n - 3)
                    nc.scalar.activation(prob[:, n % 4, :, :],
                                         ps[0:TP, 2 + n % 2, 0:2 * NQ].rearrange("p (k n) -> p k n", k=2),
                                         ACT.Exp, scale=HD ** -0.5).then_inc(exp_done, 1)
                    for m in [n - LAG] + ([n - 1, n] if n == IMG * H - 1 else []):
                        if m >= 0 and m % 4 == 3:
                            bring_group(act, m // 4)
                if kind == "D2":
                    if b:
                        read_out(act, "D3", b - 1)
                    nc.scalar.copy(oTT[:, :, :], pb).then_inc(freed_by(kind, b), 1)
                if kind == "E1":
                    if b:
                        read_out(act, "E2", b - 1)
                    nc.scalar.copy(xn2T[:, :, :], pb).then_inc(freed_by(kind, b), 1)
                if kind == "E2":
                    read_out(act, "E2", b)
                    nc.scalar.activation(pr[:, 0, :, :], lg[:, :, :], ACT.Exp).then_inc(lexp_ready, 1)
            nc.scalar.activation(warm[:, 1:2], padrow[:, 0:1], ACT.Gelu)
            for e in range(NE):
                if e == RING:
                    n = extra_tiles(act)
                act.wait_ge(ring_in[e % RING], 48 * (e // RING + 1))
                for m in range(FC):
                    act.wait_ge(w1_done, FC * e + m + 1)
                    if m == 0 and e:
                        act.wait_ge(w2_done, e)
                    nc.scalar.activation(hT[:, m, :],
                                         ps[:, (FC * e + m) % 4, 0:CAP],
                                         ACT.Gelu, bias=ring2[:, e % RING, FC * D + m:FC * D + m + 1]
                                         ).then_inc(gelu_done, 1)
            def extra_tile(i):
                for m in range(FC):
                    act.wait_ge(extra_w1, FC * i + m + 1)
                    nc.scalar.activation(hT[:, m, :], ps[:, m % 4, 0:CAP], ACT.Gelu,
                                         bias=ring2[:, 0, FC * D + m:FC * D + m + 1]).then_inc(extra_gelu, 1)

            with act.If(n > 0):
                act.wait_ge(w2_done, NE)
                extra_tile(0)
            later_tiles(act, n, extra_tile)

        @block.vector
        def _(dve):
            links = [0]

            def link(ins):
                links[0] += 1
                ins.then_inc(dve_link, 1)
                dve.wait_ge(dve_link, links[0])

            V = nc.vector
            link(V.memset(ones[:, :], 1.0))
            link(V.memset(acc[:, 0, :], 0.0))
            link(V.memset(onesb[:, :], 1.0))
            dve.wait_ge(con_in, 16)
            link(V.tensor_copy(ltb[:, :], con[0:TP, C_LT:C_LT + TP]))
            dve.wait_ge(wt_in, 16)
            V.tensor_reduce(amax[:, 1:2], wt_sb[:, :], AX, ALU.max, apply_absolute_value=True).then_inc(amax_ready, 1)
            dve.wait_ge(x_in, 16)
            V.tensor_reduce(amax[:, 0:1], x_sb[0:KC, :], AX, ALU.max, apply_absolute_value=True).then_inc(amax_ready, 1)
            dve.wait_ge(amax_turned, 1)
            link(V.tensor_reduce(qs[:, 0:1], ps[0:2, 5, 0:KC], AX, ALU.max))
            link(V.tensor_scalar(qs[:, 1:2], qs[:, 0:1], 1e-8, 1.0 / 127.0, ALU.max, ALU.mult))
            V.tensor_scalar(qs[:, 2:4], con[0:2, C_ID:C_ID + 2], qs[:, 1:2], None, ALU.mult).then_inc(scale_diag, 1)
            dve.wait_ge(scale_spread, 1)
            link(V.tensor_copy(sc[:, 0:2], ps[:, 5, 256:258]))
            link(V.tensor_tensor(sc[:, 2:3], sc[:, 0:1], sc[:, 1:2], ALU.mult))
            V.reciprocal(sc[:, 3:5], sc[:, 0:2]).then_inc(scales_ready, 1)
            dve.wait_ge(scales_ready, 1)
            quantise(V, wt_sb[:, :].rearrange("p (k n) -> p k n", k=2), wtq[:, :, :], 1, link, quantised)
            for b in range(2):
                quantise(V, image(x_sb[0:KC, :], b), xq[:, :, NQ * b:NQ * (b + 1)], 0, link, quantised)

            def embed(b):
                dve.wait_ge(tok_done, b + 1)
                V.scalar_tensor_tensor(h[:, 2 * b:2 * b + 2, :],
                                       ps[0:TP, b, 0:2 * D].rearrange("p (t d) -> p t d", t=2), sc[0:TP, 2:3],
                                       rowb[:, 0, :].unsqueeze(1).to_broadcast([TP, 2, D]),
                                       ALU.mult, ALU.add).then_inc(h_ready, 1)

            def layernorm(b, dst, done):
                for t in (2 * b, 2 * b + 1):
                    last = V.bn_stats(stats[:, t, :], h[:, t, :])
                link(last)
                for t in (2 * b, 2 * b + 1):
                    last = V.bn_aggr(mv[:, t, :], stats[:, t, :])
                link(last)
                var, y, t = nw[:, 0, :], rstd[:, 2 * b:2 * b + 2], nw[:, 1, :]
                link(V.tensor_scalar(var, mv[:, 2 * b:2 * b + 2, 1], EPS, None, ALU.add))
                link(V.tensor_scalar(t.bitcast(I32), var.bitcast(I32), 1, None, ALU.logical_shift_right))
                link(V.tensor_scalar(y.bitcast(I32), t.bitcast(I32), -1.0, float(0x5F3759DF), ALU.mult, ALU.add))
                for _ in range(3):
                    link(V.tensor_tensor(t, y, y, ALU.mult))
                    link(V.scalar_tensor_tensor(t, t, -0.5, var, ALU.mult, ALU.mult))
                    link(V.scalar_tensor_tensor(y, t, 1.5, y, ALU.add, ALU.mult))
                for t in (2 * b, 2 * b + 1):
                    V.tensor_scalar(dst[:, t, 0:D], h[:, t, :], mv[:, t, 0:1], rstd[:, t:t + 1],
                                    ALU.subtract, ALU.mult).then_inc(done, 1)

            def over_experts(ap):
                return ap.unsqueeze(2).to_broadcast([TP, 2, NE])

            def constant(c):
                return con[0:TP, c:c + NE].unsqueeze(1).to_broadcast([TP, 2, NE])

            def choose(b):
                t2 = slice(2 * b, 2 * b + 2)
                logits = ps[0:TP, bank_of("E2", b), 0:2 * NE].rearrange("p (t e) -> p t e", t=2)
                link(V.tensor_reduce(lmax[:, 0, :], logits, AX, ALU.max))
                V.tensor_tensor(lg[:, :, :], logits, over_experts(lmax[:, 0, :]),
                                ALU.subtract).then_inc(freed_by("E2", b), 1)
                dve.wait_ge(lexp_ready, b + 1)
                link(V.tensor_reduce(lmax[:, 1, :], pr[:, 0, :, :], AX, ALU.add))
                link(V.reciprocal(lmax[:, 4, :], lmax[:, 1, :]))
                link(V.tensor_tensor(pr[:, 1, :, :], pr[:, 0, :, :], over_experts(lmax[:, 4, :]), ALU.mult))
                for k in range(2):
                    top = rows[k][:, t2, D:D + 1]
                    link(V.tensor_reduce(top, pr[:, 1 + 3 * k, :, :], AX, ALU.max))
                    link(V.tensor_tensor(pr[:, 2, :, :], pr[:, 1 + 3 * k, :, :],
                                         top.to_broadcast([TP, 2, NE]), ALU.is_ge))
                    link(V.tensor_tensor(pr[:, 3, :, :], pr[:, 2, :, :], constant(C_REV), ALU.mult))
                    link(V.tensor_reduce(lmax[:, 2 + k, :], pr[:, 3, :, :], AX, ALU.max))
                    link(V.tensor_tensor(oh[:, k, t2, :], pr[:, 3, :, :], over_experts(lmax[:, 2 + k, :]),
                                         ALU.is_equal))
                    if k == 0:
                        link(V.scalar_tensor_tensor(pr[:, 4, :, :], oh[:, 0, t2, :], -2.0, pr[:, 1, :, :],
                                                    ALU.mult, ALU.add))
                V.tensor_tensor(maskb[:, :, :], oh[:, 0, t2, :], oh[:, 1, t2, :], ALU.add).then_inc(mask_ready, 1)
                dve.wait_ge(mask_ready, b + 1)
                link(V.tensor_tensor(big[:, 0, :], maskb[:, 0, :], maskb[:, 1, :], ALU.add))
                V.tensor_tensor(acc[:, b + 1, :], acc[:, b, :], big[:, 0, :], ALU.add).then_inc(acc_ready, 1)
                dve.wait_ge(acc_ready, b + 1)

            def place(b):
                t2 = slice(2 * b, 2 * b + 2)
                ranks = ps[0:TP, bank_of("E3", b), 0:2 * NE].rearrange("p (t e) -> p t e", t=2)
                link(V.tensor_scalar(big[:, :, :], ranks, float(CAP), BIG, ALU.is_ge, ALU.mult))
                V.tensor_tensor(rkv[:, t2, :], ranks, constant(C_E128), ALU.add).then_inc(freed_by("E3", b), 1)
                read_out(dve, "E3", b)
                link(V.tensor_tensor(big[:, :, :], big[:, :, :], rkv[:, t2, :], ALU.add))
                for k in range(2):
                    last = V.tensor_tensor(sel[:, k, :, :], oh[:, k, t2, :], big[:, :, :], ALU.mult)
                link(last)
                link(V.tensor_reduce(slotf[:, b, :, :], sel[:, :, :, :], AX, ALU.add))
                V.tensor_copy(slotu[:, b, :, :], slotf[:, b, :, :]).then_inc(slot_ready, 1)

            dve.wait_ge(row_in, 64)
            embed(0)
            dve.wait_ge(h_ready, 1)
            layernorm(0, xn1, xn1_ready)
            for b in range(1, IMG):
                embed(b)
            dve.wait_ge(h_ready, IMG)
            for kind, b, i in order:
                if kind == "LN":
                    layernorm(b, xn1, xn1_ready)
                if kind == "A3":
                    computed(dve, kind, b)
                    if b == 0:
                        dve.wait_ge(pool_set, 4)
                    if b >= 3:
                        dve.wait_ge(pv_done, H * (b - 2))
                    V.tensor_tensor(vaug[:, b % 3, :, :, 0:HD],
                                    ps[0:TP, bank_of(kind, b), 0:2 * D].rearrange("p (t h d) -> p t h d", t=2, h=H),
                                    rowb[:, 1, :].rearrange("p (h d) -> p h d", h=H).unsqueeze(1)
                                    .to_broadcast([TP, 2, H, HD]), ALU.add).then_inc(freed_by(kind, b), 1)
                if kind == "B":
                    n = H * b + i
                    qt, g, hp = i // 6, i // 3 % 2, i % 3
                    col = KC + G6 * g + 2 * hp
                    dve.wait_ge(s_done, n + 1)
                    V.tensor_reduce(mx[:, qt, col:col + 2],
                                    ps[0:TP, n % 2, 0:2 * NQ].rearrange("p (h n) -> p h n", h=2),
                                    AX, ALU.max).then_inc(mx_ready, 1)
                if kind == "N":
                    computed(dve, kind, b)
                    V.tensor_scalar(qaug[KC:KA, b % 3, :, :],
                                    ps[KC:KA, bank_of(kind, b), 0:NQ].unsqueeze(1).to_broadcast([H, 2, NQ]),
                                    -1.0, None, ALU.mult).then_inc(freed_by(kind, b), 1)
                if kind == "D1":
                    if b:
                        read_out(dve, "D2", b - 1)
                    for j in range(2):
                        computed(dve, kind, b, j)
                        heads = ps[0:TP, bank_of(kind, b, j), 0:3 * P].rearrange("p (h d) -> p h d", d=32)
                        link(V.reciprocal(rec[:, j, :], heads[:, :, HD]))
                        V.tensor_tensor(otok[:, j, :].rearrange("p (h d) -> p h d", h=H), heads[:, :, 0:HD],
                                        rec[:, j, :].unsqueeze(2).to_broadcast([TP, H, HD]),
                                        ALU.mult).then_inc(freed_by(kind, b, j), 1)
                if kind == "D3":
                    computed(dve, kind, b)
                    dve.wait_ge(hb_ready, b + 1)
                    V.tensor_tensor(h[:, 2 * b:2 * b + 2, :],
                                    ps[0:TP, bank_of(kind, b), 0:2 * D].rearrange("p (t d) -> p t d", t=2),
                                    h[:, 2 * b:2 * b + 2, :], ALU.add).then_inc(freed_by(kind, b), 1)
                    read_out(dve, kind, b)
                    layernorm(b, rows[0], xn2_ready)
                if kind == "E2":
                    computed(dve, kind, b)
                    choose(b)
                if kind == "E3":
                    computed(dve, kind, b)
                    place(b)

            def bring_tokens(e):
                dve.wait_ge(t_done, e + 1)
                if e >= 2:
                    dve.wait_ge(w1_done, FC * (e - 1))
                V.tensor_copy(xsT[:, e % 2, :, :],
                              ps[0:KC, 6 + e % 2, 0:2 * CAP].rearrange("p (k n) -> p k n", k=2)).then_inc(xsT_ready, 1)

            dve.wait_ge(counted, 1)
            cmp6 = extra_cmp[:, 0:NE * 6].rearrange("p (e j) -> p e j", j=6)
            V.tensor_tensor(cmp6, ps[0:TP, 5, 0:NE].unsqueeze(2).to_broadcast([TP, NE, 6]),
                                con[0:TP, C_THR:C_THR + 6].unsqueeze(1).to_broadcast([TP, NE, 6]),
                                ALU.is_gt).then_inc(counts_read, 1)

            def find_extra():
                of, upto, start = (extra_e[:, i, :] for i in range(3))
                dve.wait_ge(counts_read, 1)
                link(V.tensor_reduce(of, cmp6, AX, ALU.add))
                square = extra_cmp.rearrange("p (e f) -> p e f", e=NE)
                link(V.tensor_tensor(square, of.unsqueeze(1).to_broadcast([TP, NE, NE]),
                                     con[0:TP, C_TRI16:C_TRI16 + NE * NE].rearrange("p (e f) -> p e f", e=NE),
                                     ALU.mult))
                link(V.tensor_reduce(upto, square, AX, ALU.add))
                link(V.tensor_tensor(start, upto, of, ALU.subtract))
                link(V.scalar_tensor_tensor(start, start, float(CAP), con[0:TP, C_OVC:C_OVC + NE],
                                            ALU.mult, ALU.add))

                def all_tiles(ap):
                    return ap.unsqueeze(1).to_broadcast([TP, NT, NE])

                val, small = extra_val[:, 0, :, :], extra_val[:, 1, :, :]
                link(V.tensor_tensor(small, rkv[:, :, :], all_tiles(con[0:TP, C_E128:C_E128 + NE]), ALU.subtract))
                link(V.tensor_scalar(small, small, float(CAP), BIG, ALU.is_lt, ALU.mult))
                link(V.tensor_tensor(val, rkv[:, :, :], all_tiles(start), ALU.add))
                link(V.tensor_tensor(val, val, small, ALU.add))
                for k in range(2):
                    last = V.tensor_tensor(extra_sel[:, k, :, :], oh[:, k, :, :], val, ALU.mult)
                link(last)
                link(V.tensor_reduce(extra_slotf, extra_sel, AX, ALU.add))
                link(V.tensor_copy(extra_slot, extra_slotf))
                table = extra_cmp[0:1, 0:NOV * NE].rearrange("p (i e) -> p i e", i=NOV)
                link(V.tensor_tensor(table, upto[0:1, :].unsqueeze(1).to_broadcast([1, NOV, NE]),
                                     con[0:1, C_I12:C_I12 + NOV].unsqueeze(2).to_broadcast([1, NOV, NE]),
                                     ALU.is_le))
                link(V.tensor_reduce(extra_idf[:, 0:NOV], table, AX, ALU.add))
                link(V.tensor_scalar(extra_idf[:, 0:NOV], extra_idf[:, 0:NOV], float(NE - 1), None, ALU.min))
                link(V.tensor_copy(extra_idf[:, NOV:NOV + 1], upto[0:1, NE - 1:NE]))
                V.tensor_copy(extra_id, extra_idf).then_inc(extra_known, 1)

            bring_tokens(0)
            for e in range(NE):
                if e + 1 < NE:
                    bring_tokens(e + 1)
                if e == 0:
                    find_extra()
                if e == RING:
                    n = extra_tiles(dve)
                dve.wait_ge(w2_done, e + 1)
                dve.wait_ge(ring_in[e % RING], 48 * (e // RING + 1))
                V.tensor_tensor(eo[:, e % 2, :], ps[:, 4 + e % 2, 0:D], ringb[:, e % RING, :],
                                ALU.add).then_inc(eo_ready, 1)
                dve.wait_ge(eo_ready, e + 1)
                dve.wait_ge(xs_in[e // 4], 16)
                if e >= 2:
                    dve.wait_ge(added, 16 * (e - 1))
                V.tensor_scalar(eog[:, e % 2, :], eo[:, e % 2, :], xs[:, e, D:D + 1], None,
                                ALU.mult).then_inc(eog_ready, 1)

            def extra_tile(i):
                dve.wait_ge(extra_turned, i + 1)
                V.tensor_copy(xsT[:, 0, :, :],
                              ps[0:KC, 6, 0:2 * CAP].rearrange("p (k n) -> p k n", k=2)).then_inc(extra_x, 1)
                dve.wait_ge(extra_w2, i + 1)
                V.tensor_tensor(eo[:, 0, :], ps[:, 4, 0:D], ringb[:, 0, :], ALU.add).then_inc(extra_sum, 1)
                dve.wait_ge(extra_sum, i + 1)
                V.tensor_scalar(eog[:, 0, :], eo[:, 0, :], xs[:, 0, D:D + 1], None,
                                ALU.mult).then_inc(extra_out, 1)

            with dve.If(n > 0):
                dve.wait_ge(added, 16 * (NE - 1))
                extra_tile(0)
            later_tiles(dve, n, extra_tile)

        @block.tensor
        def _(pe):
            mm, tr = nc.tensor.matmul, nc.tensor.transpose
            def stay_awake(count):
                for _ in range(count):
                    mm(ps[:, 5, :], wtq[:, 0, 0:P], xq[:, 0, 0:512], start=True, stop=True)

            pe.wait_ge(con_in, 16)
            pe.wait_ge(amax_ready, 2)
            tr(ps[0:2, 5, 0:KC], amax[:, :], ident[0:KC, 0:KC]).then_inc(amax_turned, 1)
            pe.wait_ge(scale_diag, 1)
            mm(ps[:, 5, 256:258], ones[0:2, :], qs[:, 2:4], start=True, stop=True).then_inc(scale_spread, 1)
            pe.wait_ge(quantised, 1)
            for t in range(NT):
                if t < 4 and t % 2 == 0:
                    pe.wait_ge(quantised, t // 2 + 2)
                if t == 4 or t == 6:
                    pe.wait_ge(quantised_pool, t // 2 - 1)
                for k in range(2):
                    last = mm(ps[0:TP, t // 2, D * (t % 2):D * (t % 2 + 1)], xq[:, k, TP * t:TP * (t + 1)],
                              wtq[:, k, :], start=(k == 0), stop=(k == 1))
                if t % 2:
                    last.then_inc(tok_done, 1)
            stay_awake(10)
            pe.wait_ge(small_in, 48)

            def values(n):
                b, hd = n // H, n % H
                pe.wait_ge(exp_done, n + 1)
                if hd == 0:
                    read_out(pe, "A3", b)
                if n == 0:
                    pe.wait_ge(pool_set, 4)
                group = n // 4
                if group >= 2 and n % 4 == 0:
                    pe.wait_ge(oT_ready, group - 1)
                for kt in range(2):
                    last = mm(ps[32 * (n % 4):32 * (n % 4) + 32, 4 + group % 2, 0:NQ],
                              vaug[:, b % 3, kt, hd, :], prob[:, n % 4, kt, :], start=(kt == 0), stop=(kt == 1),
                              skip_group_check=True)
                last.then_inc(pv_done, 1)

            pe.wait_ge(h_ready, IMG)
            for kind, b, s in order:
                if kind in ("A1", "A2q", "A2k", "A3", "N", "D2", "D3", "E1", "E2", "E3"):
                    bank_is_free(pe, kind, b)
                    bank = bank_of(kind, b)
                if kind == "A1":
                    pe.wait_ge(xn1_ready, 2 * (b + 1))
                    for k in range(2):
                        for t in range(2):
                            last = tr(ps[0:KC, bank, NQ * k + TP * t:NQ * k + TP * (t + 1)],
                                      xn1[:, 2 * b + t, KC * k:KC * (k + 1)], ident[0:TP, 0:TP])
                    last.then_inc(misc_ready, 1)
                if kind in ("A2q", "A2k"):
                    if kind == "A2q":
                        read_out(pe, "A1", b)
                    at = 0 if kind == "A2q" else D
                    for g in range(2):
                        for k in range(2):
                            last = mm(ps[0:KC, bank, NQ * g:NQ * (g + 1)],
                                      wqkv_sb[:, k, at + KC * g:at + KC * (g + 1)], xnT[:, k, :],
                                      start=(k == 0), stop=(k == 1))
                    last.then_inc(misc_ready, 1)
                if kind == "A3":
                    for t in range(2):
                        for k in range(2):
                            last = mm(ps[0:TP, bank, D * t:D * (t + 1)], xnT[:, k, TP * t:TP * (t + 1)],
                                      wqkv_sb[:, k, 2 * D:3 * D], start=(k == 0), stop=(k == 1))
                    last.then_inc(misc_ready, 1)
                if kind == "B":
                    n = H * b + s
                    qt, g, hp = s // 6, s // 3 % 2, s % 3
                    if s == 0:
                        read_out(pe, "A2q", b)
                    if s % 6 in (0, 3):
                        pe.wait_ge(kmb_ready, 2 * b + g + 1)
                    if n >= 2:
                        pe.wait_ge(mx_ready, n - 1)
                    hd = G6 * g + 2 * hp
                    mm(ps[0:TP, n % 2, 0:2 * NQ], qbf[:, b % 2, g, TP * qt:TP * (qt + 1)],
                       kmb[:, b % 2, hd:hd + 2, :].rearrange("p h n -> p (h n)"),
                       start=True, stop=True).then_inc(s_done, 1)
                if kind == "N":
                    pe.wait_ge(mx_ready, H * (b + 1))
                    pe.wait_ge(pool_set, 5)
                    for t in range(2):
                        last = mm(ps[0:KA, bank, TP * t:TP * (t + 1)], mx[:, t, 0:KA], ident[0:TP, 0:TP],
                                  start=True, stop=True)
                    last.then_inc(misc_ready, 1)
                if kind == "C":
                    n = H * b + s
                    if s == 0:
                        read_out(pe, "N", b)
                        pe.wait_ge(kmask_ready, 2 * (b + 1))
                    if n == 0:
                        pe.wait_ge(own_in, 48)
                    if n >= 2:
                        pe.wait_ge(exp_done, n - 1)
                    for kt in range(2):
                        last = mm(ps[0:TP, 2 + n % 2, NQ * kt:NQ * (kt + 1)],
                                  kmask[:, b % 3, s, TP * kt:TP * (kt + 1)], qaug[:, b % 3, s // G6, :],
                                  start=True, stop=True)
                    last.then_inc(st_done, 1)
                    if n >= LAG:
                        values(n - LAG)
                    if n == IMG * H - 1:
                        values(n - 1)
                        values(n)
                if kind == "D1":
                    pe.wait_ge(oT_ready, 3 * (b + 1))
                    for t in range(2):
                        bank_is_free(pe, kind, b, t)
                        for r in range(3):
                            last = tr(ps[0:TP, bank_of(kind, b, t), P * r:P * (r + 1)],
                                      oT[:, b % 2, r, TP * t:TP * (t + 1)], ident)
                        last.then_inc(misc_ready, 1)
                if kind == "D2":
                    read_out(pe, "D1", b, 0)
                    read_out(pe, "D1", b, 1)
                    for k in range(2):
                        for t in range(2):
                            last = tr(ps[0:KC, bank, NQ * k + TP * t:NQ * k + TP * (t + 1)],
                                      otok[:, t, KC * k:KC * (k + 1)], ident[0:TP, 0:TP])
                    last.then_inc(misc_ready, 1)
                if kind == "D3":
                    read_out(pe, "D2", b)
                    for t in range(2):
                        for k in range(2):
                            last = mm(ps[0:TP, bank, D * t:D * (t + 1)], oTT[:, k, TP * t:TP * (t + 1)],
                                      wo_sb[:, k, :], start=(k == 0), stop=(k == 1))
                    last.then_inc(misc_ready, 1)
                if kind == "E1":
                    pe.wait_ge(xn2_ready, 2 * (b + 1))
                    for k in range(2):
                        for t in range(2):
                            last = tr(ps[0:KC, bank, NQ * k + TP * t:NQ * k + TP * (t + 1)],
                                      rows[0][:, 2 * b + t, KC * k:KC * (k + 1)], ident[0:TP, 0:TP])
                    last.then_inc(misc_ready, 1)
                if kind == "E2":
                    read_out(pe, "E1", b)
                    for t in range(2):
                        for k in range(2):
                            last = mm(ps[0:TP, bank, NE * t:NE * (t + 1)], xn2T[:, k, TP * t:TP * (t + 1)],
                                      wr_sb[:, k, :], start=(k == 0), stop=(k == 1))
                    last.then_inc(misc_ready, 1)
                if kind == "E3":
                    pe.wait_ge(mask_ready, b + 1)
                    mm(ps[0:TP, bank, 0:NE], ltb[:, :], maskb[:, 0, :], start=True, stop=False)
                    mm(ps[0:TP, bank, 0:NE], onesb[:, :], acc[:, b, :], start=False, stop=True)
                    mm(ps[0:TP, bank, NE:2 * NE], ltb[:, :], maskb[:, 1, :], start=True, stop=False)
                    mm(ps[0:TP, bank, NE:2 * NE], onesb[:, :], maskb[:, 0, :], start=False, stop=False)
                    mm(ps[0:TP, bank, NE:2 * NE], onesb[:, :], acc[:, b, :], start=False,
                       stop=True).then_inc(misc_ready, 1)

            pe.wait_ge(acc_ready, IMG)
            mm(ps[0:TP, 5, 0:NE], onesb[:, :], acc[:, IMG, :], start=True, stop=True).then_inc(counted, 1)

            pe.wait_ge(counts_read, 1)
            stay_awake(30)

            def turn_tokens(e):
                pe.wait_ge(xs_in[e // 4], 16)
                if e >= 2:
                    pe.wait_ge(xsT_ready, e - 1)
                for k in range(2):
                    last = tr(ps[0:KC, 6 + e % 2, CAP * k:CAP * (k + 1)], xs[:, e, KC * k:KC * (k + 1)], ident)
                last.then_inc(t_done, 1)

            turn_tokens(0)
            for e in range(NE):
                r = e % RING
                if e == RING:
                    n = extra_tiles(pe)
                pe.wait_ge(ring_in[r], 48 * (e // RING + 1))
                pe.wait_ge(xsT_ready, e + 1)
                for m in range(FC):
                    if FC * e + m >= 4:
                        pe.wait_ge(gelu_done, FC * e + m - 3)
                    for k in range(2):
                        last = mm(ps[:, (FC * e + m) % 4, 0:CAP],
                                  ring1[:, r, FF * k + P * m:FF * k + P * (m + 1)], xsT[:, e % 2, k, :],
                                  start=(k == 0), stop=(k == 1))
                    last.then_inc(w1_done, 1)
                if e + 1 < NE:
                    turn_tokens(e + 1)
                if e >= 2:
                    pe.wait_ge(eo_ready, e - 1)
                for m in range(FC):
                    pe.wait_ge(gelu_done, FC * e + m + 1)
                    last = mm(ps[:, 4 + e % 2, 0:D], hT[:, m, :], ring2[:, r, D * m:D * (m + 1)],
                              start=(m == 0), stop=(m == FC - 1))
                last.then_inc(w2_done, 1)

            def extra_tile(i):
                pe.wait_ge(extra_in, 64 * i + 64)
                for k in range(2):
                    last = tr(ps[0:KC, 6, CAP * k:CAP * (k + 1)], xs[:, 0, KC * k:KC * (k + 1)], ident)
                last.then_inc(extra_turned, 1)
                pe.wait_ge(extra_x, i + 1)
                for m in range(FC):
                    if m >= 4:
                        pe.wait_ge(extra_gelu, FC * i + m - 3)
                    for k in range(2):
                        last = mm(ps[:, m % 4, 0:CAP], ring1[:, 0, FF * k + P * m:FF * k + P * (m + 1)],
                                  xsT[:, 0, k, :], start=(k == 0), stop=(k == 1))
                    last.then_inc(extra_w1, 1)
                for m in range(FC):
                    pe.wait_ge(extra_gelu, FC * i + m + 1)
                    last = mm(ps[:, 4, 0:D], hT[:, m, :], ring2[:, 0, D * m:D * (m + 1)],
                              start=(m == 0), stop=(m == FC - 1))
                last.then_inc(extra_w2, 1)

            with pe.If(n > 0):
                pe.wait_ge(gelu_done, FC * NE)
                pe.wait_ge(eo_ready, NE - 1)
                extra_tile(0)
            later_tiles(pe, n, extra_tile)


def constants():
    import numpy as np
    c = np.zeros((P, C_N), np.float32)
    p = np.arange(P)
    c[:, C_ID:C_ID + P] = np.eye(P)
    for j in range(H):
        c[:KC, C_HM + j] = (p[:KC] // HD == j)
        c[KC + j, C_HM + j] = 1
    e = np.arange(NE)
    c[:, C_REV:C_REV + NE] = NE - e
    c[:, C_E128:C_E128 + NE] = CAP * e
    c[:, C_THR:C_THR + 6] = CAP * np.arange(1, 7)
    c[:, C_TRI16:C_TRI16 + NE * NE] = (e[None, :] <= e[:, None]).reshape(-1)
    c[:, C_OVC:C_OVC + NE] = (NE - 1) * CAP - CAP * e
    c[:, C_I12:C_I12 + NOV] = np.arange(NOV)
    c[:, C_LT:C_LT + TP] = p[:, None] < np.arange(TP)[None, :]
    return c


def kernel(**inputs):
    import numpy as np
    import concourse.bacc as bacc
    from concourse import mybir as mb
    from concourse.bass_utils import run_bass_kernel_spmd as run

    a = {k: np.asarray(v) for k, v in inputs.items()}
    def chunks(m):
        return m.reshape(2, KC, m.shape[1]).transpose(1, 0, 2)

    x = a["x"].reshape(IMG, 3, 14, 8, 14, 8).transpose(1, 3, 5, 0, 2, 4).reshape(D, TOK)
    w1 = a["L0_ffn_W1"].reshape(NE, 2, KC, FF).transpose(0, 2, 1, 3).reshape(NE, KC, 2 * FF)
    w2 = a["L0_ffn_W2"].reshape(NE, FC, P, D).transpose(0, 2, 1, 3).reshape(NE, P, FC * D)
    b1 = a["L0_ffn_b1"].reshape(NE, FC, P).transpose(0, 2, 1)
    qkv_b = a["L0_attn_qkv_b"]
    data = {
        "xp": chunks(x).reshape(KC, 2 * TOK),
        "wtok": chunks(a["L0_tok_w"].reshape(D, D).T).reshape(KC, 2 * D),
        "tokb": a["L0_tok_b"].reshape(1, D),
        "wqkv": chunks(a["L0_attn_qkv_w"].T),
        "qkb": qkv_b[:2 * D].reshape(4, KC).T,
        "vb": qkv_b[2 * D:].reshape(1, D),
        "wout": chunks(a["L0_attn_out_w"].T),
        "outb": a["L0_attn_out_b"].reshape(1, D),
        "wr": chunks(a["L0_ffn_Wr"].T),
        "w1": w1,
        "w2": np.concatenate([w2, b1], axis=2),
        "b2": a["L0_ffn_b2"],
        "consts": constants(),
        "own": np.repeat(np.eye(H, dtype=np.float32), NQ, axis=1).reshape(H, H, NQ),
    }
    nc = bacc.Bacc("TRN2", target_bir_lowering=False, num_devices=1)
    arrays, args = {}, []
    for name, v in data.items():
        v = np.ascontiguousarray(v)
        arrays[name] = v
        args.append(nc.dram_tensor(name, v.shape, mb.dt.from_np(v.dtype), kind="ExternalInput").ap())
    args.append(nc.dram_tensor("out", (TOK + P, D), mb.dt.float32, kind="ExternalOutput").ap())
    vit_block(nc, *args)
    r = run(nc, [arrays], core_ids=[0])
    return r.results[0]["out"][:TOK].reshape(IMG, NQ, D)
```

```python
from contextlib import ExitStack

import concourse.bass as bass
from concourse import mybir

F32 = mybir.dt.float32
BF16 = mybir.dt.bfloat16
U32 = mybir.dt.uint32
I32 = mybir.dt.int32
ALU = mybir.AluOpType
ACT = mybir.ActivationFunctionType
AX = mybir.AxisListType.X

P = 128
IMG = 4
TP = 98
NQ = 2 * TP
NT = 2 * IMG
TOK = NT * TP
D = 192
KC = 96
H, HD = 12, 16
G6 = 6
QK = ("query", "key")
PARTS = 3
STACK = (((0, 1, 0), (1, 1, 0), (2, 1, 0), (3, 1, 1), (4, 1, 1), (5, 1, 2)),
         ((0, 3, 0), (3, 2, 0), (5, 1, 0)))
KA = KC + 2
NE, FF = 16, 768
FC = FF // P
CAP = P
NOV = 12
ROW = D + 2
RING = 8
W2R = FC * D + FC
XS_LOADS = ((0, 1), (1, 4), (4, 10), (10, 16))
AWAKE = {("A1", 0): 2, ("A3", 0): 4, ("A1", 1): 2, ("A3", 1): 8,
         ("D1", 3): 2, ("D2", 3): 3, ("D3", 3): 22, ("E1", 3): 3, ("E2", 3): 12}
AWAKE_MAXIMA = (1, 0, 0, 0)
AWAKE_SCORES = 1
AWAKE_LAST_SCORES = 2
AWAKE_TOKENS = 16
AWAKE_COUNTS = 26
WARM_SCALES = 2
LAG = 2
MAGIC = 12582912.0
BIG = 65536.0
LARGE = 1e30
EPS = 1e-5

C_ID, C_MAGIC, C_REV, C_E128, C_THR, C_TRI16, C_OVC, C_I12, C_LT = 0, 128, 140, 156, 172, 178, 434, 450, 462
C_N = C_LT + TP


def schedule():
    order = [(kind, b, 0) for b in range(2) for kind in ("A1", "A2q", "A2k", "A3")]
    for b in range(-1, IMG + 1):
        if b == -1:
            beside = {0: [("A1", 2)], 2: [("A2q", 2)], 6: [("N", 0), ("M", 0), ("A2k", 2), ("A3", 2)]}
        elif b < IMG - 1:
            beside = {0: [("E1", b - 2)], 2: [("D1", b - 1)], 4: [("D2", b - 1)],
                      6: [("N", b + 1), ("D3", b - 1)], 7: [("M", b + 1), ("E2", b - 2)],
                      9: [("G", b - 2)], 10: [("L", b - 1)], 11: [("E3", b - 2)]}
        elif b < IMG:
            beside = {2: [("E1", b - 2), ("D1", b - 1)], 3: [("E2", b - 2)], 4: [("D2", b - 1)],
                      5: [("G", b - 2)], 6: [("E3", b - 2), ("D3", b - 1), ("L", b - 1)],
                      11: [("E1", b - 1)]}
        else:
            beside = {0: [("D1", b - 1), ("E2", b - 2), ("D2", b - 1), ("G", b - 2), ("D3", b - 1),
                          ("L", b - 1), ("E1", b - 1), ("E3", b - 2)]}
        if b == 0:
            beside.update({0: [("A1", 3)], 2: [("A2q", 3)], 4: [("A2k", 3)]})
        for s in range(H):
            if 0 <= b < IMG:
                order.append(("C", b, s))
            if b + 1 < IMG and s < H // 2:
                order += [("B", b + 1, 2 * s), ("B", b + 1, 2 * s + 1)]
            order += [(kind, c, 0) for kind, c in beside.get(s, []) if 0 <= c < IMG]
            if b == 1 and s == 2:
                order.append(("A3", 3, 0))
    order += [("E2", IMG - 1, 0), ("G", IMG - 1, 0), ("E3", IMG - 1, 0)]
    return order


def vit_block(nc, xp, wtok, tokb, wqkv, qkb, vb, wout, outb, wr, w1, w2, b2, consts, out):
    order = schedule()
    pieces = []
    for kind, b, _ in order:
        if kind == "D1":
            pieces += [("D1", b, 0), ("D1", b, 1)]
        elif kind not in ("B", "C", "M", "L", "G"):
            pieces.append((kind, b, 0))
    piece = {p: n for n, p in enumerate(pieces)}

    with ExitStack() as ctx:
        def sb(name, shape, dt=F32):
            return ctx.enter_context(nc.sbuf_tensor(name, shape, dt))

        def sem(name):
            return ctx.enter_context(nc.semaphore(name))

        ps = ctx.enter_context(nc.psum_tensor("ps", [P, 8, 512], F32))
        slots = nc.dram_tensor("slots", ((NE + NOV) * CAP, ROW), F32, kind="Internal").ap()

        parts_out = nc.dram_tensor("parts_out", (IMG, 2, 2, PARTS * KC, NQ), BF16, kind="Internal").ap()

        con = sb("con", [P, C_N])
        x_sb = sb("x_sb", [TP, 2 * TOK])
        warm = sb("warm", [P, 2])
        xq = sb("xq", [KC, 2, TOK], BF16)
        wt_sb = sb("wt_sb", [KC, 2 * D])
        wtq = sb("wtq", [KC, 2, D], BF16)
        amax = sb("amax", [KC, 2])
        qs = sb("qs", [2, 4])
        sc = sb("sc", [P, 5])
        ones = sb("ones", [P, P])
        onesb = sb("onesb", [TP, TP], BF16)
        ltb = sb("ltb", [TP, TP], BF16)
        wqkv_sb = sb("wqkv_sb", [KC, 2, 3 * D])
        wo_sb = sb("wo_sb", [KC, 2, D])
        wr_sb = sb("wr_sb", [KC, 2, NE])
        qkb_sb = sb("qkb_sb", [KC, 4])
        rowb = sb("rowb", [TP, 3, D])
        h = sb("h", [TP, NT, D])
        stats = sb("stats", [TP, NT, 6])
        mv = sb("mv", [TP, NT, 2])
        rstd = sb("rstd", [TP, NT])
        nw = sb("nw", [TP, 2, NT])
        xn1 = sb("xn1", [TP, NT, D])
        xnT = sb("xnT", [KC, 2, NQ])
        qk = sb("qk", [KC, 2, 2, NQ])
        parts = sb("parts", [KC, 2, 2, PARTS, NQ], BF16)
        room = sb("room", [P, 3 * H * NQ])
        qst, kst = (room[0:KA, 3 * H * NQ // 2 * i:3 * H * NQ // 2 * (i + 1)].bitcast(BF16)
                    .rearrange("p (b h n) -> p b h n", b=3, h=H) for i in range(2))
        vaug = sb("vaug", [TP, 3, 2, H, 32])
        mx = sb("mx", [TP, 2, H])
        mxp = sb("mxp", [H, 2, NQ], BF16)
        prob = x_sb[:, 0:4 * 2 * NQ].rearrange("p (b k n) -> p b k n", b=4, k=2)
        oT = sb("oT", [P, 2, 3, NQ])
        rec = sb("rec", [TP, 2, H])
        otok = sb("otok", [TP, 2, D])
        oTT = sb("oTT", [KC, 2, NQ])
        rows = [sb(f"rows{k}", [TP, NT, ROW]) for k in range(2)]
        base = xn1
        xn2T = sb("xn2T", [KC, 2, NQ])
        lg = sb("lg", [TP, 2, NE])
        top, top_mark, second, second_mark, lsum, second_exp = (
            sb(n, [TP, 2]) for n in ("top", "top_mark", "second", "second_mark", "lsum", "second_exp"))
        lexp, top_sel, others, second_sel = (
            sb(n, [TP, 2, NE]) for n in ("lexp", "top_sel", "others", "second_sel"))
        oh = sb("oh", [TP, 2, NT, NE])
        maskb = sb("maskb", [TP, 2, NE], BF16)
        acc = sb("acc", [TP, IMG + 1, NE], BF16)
        rkv = sb("rkv", [TP, NT, NE])
        big = sb("big", [TP, 2, NE])
        sel = sb("sel", [TP, 2, 2, NE])
        slotf = sb("slotf", [TP, IMG, 2, 2])
        slotu = sb("slotu", [TP, IMG, 2, 2], U32)
        tokid = sb("tokid", [TP, NT], U32)
        padrow = sb("padrow", [P, ROW])
        ring1 = sb("ring1", [KC, RING, 2 * FF])
        ring2 = sb("ring2", [P, RING, W2R])
        ringb = sb("ringb", [P, RING, D])
        taken = [0]

        def view(width):
            taken[0] += width
            return room[:, taken[0] - width:taken[0]]

        xs = view(NE * ROW).rearrange("p (e c) -> p e c", e=NE)
        xsT = view(4 * CAP)[0:KC, :].rearrange("p (b k n) -> p b k n", b=2, k=2)
        hT = view(FC * CAP).rearrange("p (m n) -> p m n", m=FC)
        eo = view(2 * D).rearrange("p (b d) -> p b d", b=2)
        eog = view(2 * D).rearrange("p (b d) -> p b d", b=2)
        extra_cmp = view(NE * NE)[0:TP, :]
        extra_e = view(3 * NE)[0:TP, :].rearrange("p (i e) -> p i e", i=3)
        extra_val = view(2 * NT * NE)[0:TP, :].rearrange("p (i t e) -> p i t e", i=2, t=NT)
        extra_sel = view(2 * NT * NE)[0:TP, :].rearrange("p (k t e) -> p k t e", k=2, t=NT)
        extra_slotf = view(2 * NT)[0:TP, :].rearrange("p (k t) -> p k t", k=2)
        extra_slot = view(2 * NT)[0:TP, :].bitcast(U32).rearrange("p (k t) -> p k t", k=2)
        extra_idf = view(NOV + 1)[0:1, :]
        extra_id = view(NOV + 1)[0:1, :].bitcast(I32)

        ident = con[:, C_ID:C_ID + P]

        con_in, x_in, wt_in, small_in, row_in, pad_in = (sem(n) for n in
            ("con_in", "x_in", "wt_in", "small_in", "row_in", "pad_in"))
        ring_in = [sem(f"ring_in{i}") for i in range(RING)]
        scales_ready, clipped, weights_quantised = sem("scales_ready"), sem("clipped"), sem("weights_quantised")
        dve_link, pool_link = sem("dve_link"), sem("pool_link")
        pool_set = sem("pool_set")
        amax_ready, amax_turned, scale_diag, scale_spread, quantised = (sem(n) for n in
            ("amax_ready", "amax_turned", "scale_diag", "scale_spread", "quantised"))
        tok_done, h_ready, xn1_ready = sem("tok_done"), sem("h_ready"), sem("xn1_ready")
        misc_ready = sem("misc_ready")
        bank_read = [sem(f"bank_read{i}") for i in range(2)]
        hb_ready, moments_ready, rstd_ready = sem("hb_ready"), sem("moments_ready"), sem("rstd_ready")
        whole_ready, parts_ready, parts_stored, stack_in = ([sem(f"{n}_{i}") for i in QK] for n in
            ("whole_ready", "parts_ready", "parts_stored", "stack_in"))
        mxp_ready, mxp_in = sem("mxp_ready"), sem("mxp_in")
        s_done, mx_ready = sem("s_done"), sem("mx_ready")
        st_done, exp_done, pv_done, oT_ready = (sem(n) for n in ("st_done", "exp_done", "pv_done", "oT_ready"))
        xn2_ready, lexp_ready, mask_ready, slot_ready, base_ready, rows_ready = (sem(n) for n in
            ("xn2_ready", "lexp_ready", "mask_ready", "slot_ready", "base_ready", "rows_ready"))
        base_out, scattered = sem("base_out"), sem("scattered")
        xs_in = [sem(f"xs_in{i}") for i in range(len(XS_LOADS))]
        t_done, xsT_ready, w1_done, gelu_done, w2_done, eo_ready, eog_ready = (sem(n) for n in
            ("t_done", "xsT_ready", "w1_done", "gelu_done", "w2_done", "eo_ready", "eog_ready"))
        added = sem("added")
        acc_ready, counted, counts_read, extra_known, extra_scattered = (sem(n) for n in
            ("acc_ready", "counted", "counts_read", "extra_known", "extra_scattered"))
        extra_seen = sem("extra_seen")
        second_known, second_ready, gates_ready = sem("second_known"), sem("second_ready"), sem("gates_ready")
        extra_in, extra_turned, extra_x, extra_w1, extra_gelu, extra_w2, extra_sum, extra_out, extra_added = (
            sem(n) for n in ("extra_in", "extra_turned", "extra_x", "extra_w1", "extra_gelu", "extra_w2",
                             "extra_sum", "extra_out", "extra_added"))

        out_rows = out[0:TOK, :]

        def load_of(e):
            return next(i for i, (first, end) in enumerate(XS_LOADS) if first <= e < end)

        block = ctx.enter_context(nc.Block())

        def bank_of(kind, b, i=0):
            return 6 + piece[(kind, b, i)] % 2

        def bank_is_free(pe, kind, b, i=0):
            n = piece[(kind, b, i)]
            if n >= 2:
                pe.wait_ge(bank_read[n % 2], n // 2)

        def computed(eng, kind, b, i=0):
            eng.wait_ge(misc_ready, piece[(kind, b, i)] + 1)

        def read_out(eng, kind, b, i=0):
            n = piece[(kind, b, i)]
            eng.wait_ge(bank_read[n % 2], n // 2 + 1)

        def freed_by(kind, b, i=0):
            return bank_read[piece[(kind, b, i)] % 2]

        def extra_tiles(eng):
            eng.wait_ge(extra_known, 1)
            return eng.value_load(extra_id[0:1, NOV:NOV + 1], min_val=0, max_val=NOV)

        def later_tiles(eng, n, tile):
            with eng.If(n > 1):
                with eng.Fori(1, NOV) as i:
                    with eng.If(i < n):
                        tile(i)

        @block.sync
        def _(sp):
            sp.dma_start(x_sb[0:KC, :], xp).then_inc(x_in, 16)
            sp.dma_start(wt_sb[:, :], wtok).then_inc(wt_in, 16)
            sp.dma_start(wqkv_sb[:, :, :], wqkv).then_inc(small_in, 16)
            sp.dma_start(wo_sb[:, :, :], wout).then_inc(small_in, 16)
            sp.dma_start(wr_sb[:, :, :], wr).then_inc(small_in, 16)

            def load_first(e):
                r = e % RING
                sp.dma_start(ring1[:, r, :], w1[e]).then_inc(ring_in[r], 16)

            def load_second(e):
                r = e % RING
                sp.dma_start(ring2[:, r, :], w2[e]).then_inc(ring_in[r], 16)
                sp.dma_start(ringb[:, r, :], b2[e:e + 1, :].to_broadcast([P, D])).then_inc(ring_in[r], 16)

            def restack(b):
                for i, name in enumerate(QK):
                    sp.wait_ge(parts_ready[i], b + 1)
                    sp.dma_start(parts_out[b, i].rearrange("g (p f) n -> f g p n", p=PARTS),
                                 parts[:, i, :, :, :]).then_inc(parts_stored[i], 16)
                if b >= 3:
                    sp.wait_ge(st_done, H * (b - 2))
                for i, stack in ((0, qst), (1, kst)):
                    sp.wait_ge(parts_stored[i], 16 * (b + 1))
                    for row, many, part in STACK[i]:
                        sp.dma_start(stack[HD * row:HD * (row + many), b % 3, :, :]
                                     .rearrange("p (g h) n -> p g (h n)", g=2),
                                     parts_out[b, i, :, KC * part:KC * (part + many), :]
                                     .rearrange("g (f h) n -> f g (h n)", h=G6)).then_inc(stack_in[i], 16)

            for kind, b, s in order:
                if kind == "A2k":
                    restack(b)
                if kind == "C" and s % 3 == 1:
                    sp.wait_ge(st_done, H * b + s)
                    if s % 2:
                        load_first(2 * b + s // 6)
                    else:
                        load_second(2 * b + s // 6)
                if kind == "E1":
                    sp.wait_ge(base_ready, b + 1)
                    sp.dma_start(out_rows[NQ * b:NQ * (b + 1), :].rearrange("(t p) d -> p t d", p=TP),
                                 base[:, 2 * b:2 * b + 2, :]).then_inc(base_out, 16)
            sp.wait_ge(scattered, 16 * 2 * NT)
            for i, (first, end) in enumerate(XS_LOADS):
                sp.dma_start(xs[:, first:end, :],
                             slots[first * CAP:end * CAP, :].rearrange("(e p) c -> p e c", p=CAP)
                             ).then_inc(xs_in[i], 16)
            for e in range(RING, NE):
                sp.wait_ge(eo_ready, e - RING + 1)
                load_first(e)
                load_second(e)

            def load_extra(i):
                e = sp.value_load(extra_id[0:1, bass.ds(i, 1)], min_val=0, max_val=NE - 1)
                sp.dma_start(ring1[:, 0, :], w1[bass.ds(e, 1), :, :].rearrange("e p f -> (e p) f")
                             ).then_inc(extra_in, 16)
                sp.dma_start(ring2[:, 0, :], w2[bass.ds(e, 1), :, :].rearrange("e p f -> (e p) f")
                             ).then_inc(extra_in, 16)
                sp.dma_start(ringb[:, 0, :], b2[bass.ds(e, 1), :].to_broadcast([P, D])).then_inc(extra_in, 16)
                sp.dma_start(xs[:, 0, :], slots[bass.ds(i * CAP + NE * CAP, CAP), :]).then_inc(extra_in, 16)

            n = extra_tiles(sp)
            with sp.If(n > 0):
                sp.wait_ge(eo_ready, RING + 1)
                sp.wait_ge(added, 16)
                sp.wait_ge(extra_scattered, 16 * 2 * NT)
                load_extra(0)

            def extra_tile(i):
                sp.wait_ge(extra_added, 16 * i)
                load_extra(i)

            later_tiles(sp, n, extra_tile)

        def image(ap, b):
            return ap.rearrange("p (k n) -> p k n", k=2)[:, :, NQ * b:NQ * (b + 1)]

        def first_guess(engine, tiles, link):
            some = slice(tiles[0], tiles[-1] + 1)
            var, y = nw[:, 0, some], rstd[:, some]
            link(engine.tensor_scalar(var, mv[:, some, 1], EPS, None, ALU.add))
            link(engine.tensor_scalar(y.bitcast(I32), var.bitcast(I32), -0.5, float(0x5F3759DF),
                                      ALU.mult, ALU.add))
            return var, y, nw[:, 1, some]

        def split(engine, i, link):
            engine.tensor_tensor(parts[:, i, :, 1, :], qk[:, i, :, :], parts[:, i, :, 0, :], ALU.subtract)
            link(engine.tensor_tensor(qk[:, i, :, :], qk[:, i, :, :], parts[:, i, :, 0, :], ALU.subtract))
            engine.tensor_tensor(parts[:, i, :, 2, :], qk[:, i, :, :], parts[:, i, :, 1, :],
                                 ALU.subtract).then_inc(parts_ready[i], 1)

        @block.gpsimd
        def _(pool):
            nc.gpsimd.iota(tokid[:, :], pattern=[[TP, NT]], base=0, channel_multiplier=1).then_inc(pool_link, 1)
            nc.gpsimd.memset(padrow[:, 0:ROW - 1], 0.0).then_inc(pool_link, 1)
            nc.gpsimd.iota(padrow[:, ROW - 1:ROW].bitcast(U32), pattern=[[0, 1]], base=TOK,
                           channel_multiplier=1).then_inc(pool_set, 1)
            pool.wait_ge(pool_link, 1)
            for k in range(2):
                nc.gpsimd.tensor_copy(rows[k][:, :, ROW - 1:ROW].bitcast(U32),
                                      tokid[:, :].unsqueeze(2)).then_inc(pool_set, 1)
            nc.gpsimd.memset(vaug[:, :, :, :, HD:32], 1.0).then_inc(pool_set, 1)
            pool.wait_ge(pool_set, 4)
            nc.gpsimd.memset(kst[KC:KA, :, :, :], 1.0).then_inc(pool_set, 1)
            pool.wait_ge(pool_set, 5)
            pool_links = [2]

            def link(ins):
                pool_links[0] += 1
                ins.then_inc(pool_link, 1)
                pool.wait_ge(pool_link, pool_links[0])

            pool.wait_ge(row_in, 64)
            for kind, b, _ in order:
                if kind == "A1":
                    pool.wait_ge(xn1_ready, 2 * (b + 1))
                    nc.gpsimd.tensor_tensor(h[:, 2 * b:2 * b + 2, :], h[:, 2 * b:2 * b + 2, :],
                                            rowb[:, 2, :].unsqueeze(1).to_broadcast([TP, 2, D]),
                                            ALU.add).then_inc(hb_ready, 1)
                if kind == "A2k":
                    for i in range(2):
                        if b or i == 0:
                            pool.wait_ge(whole_ready[i], b + 1)
                            split(nc.gpsimd, i, link)
                if kind == "D3" and b < IMG - 2:
                    pool.wait_ge(moments_ready, b + 1)
                    var, y, t = first_guess(nc.gpsimd, range(2 * b, 2 * b + 2), link)
                    for step in range(3):
                        link(nc.gpsimd.tensor_tensor(t, y, y, ALU.mult))
                        link(nc.gpsimd.tensor_tensor(t, t, var, ALU.mult))
                        link(nc.gpsimd.tensor_scalar(t, t, -0.5, 1.5, ALU.mult, ALU.add))
                        last = nc.gpsimd.tensor_tensor(y, t, y, ALU.mult)
                        if step < 2:
                            link(last)
                    last.then_inc(rstd_ready, 1)
                if kind == "E1":
                    pool.wait_ge(xn2_ready, 2 * (b + 1))
                    nc.gpsimd.tensor_copy(rows[1][:, 2 * b:2 * b + 2, 0:D],
                                          rows[0][:, 2 * b:2 * b + 2, 0:D]).then_inc(rows_ready, 1)
                    nc.gpsimd.tensor_tensor(base[:, 2 * b:2 * b + 2, :], h[:, 2 * b:2 * b + 2, :],
                                            rows[0][:, 2 * b:2 * b + 2, 0:D], ALU.add).then_inc(base_ready, 1)
                if kind == "E3":
                    if b == 0:
                        pool.wait_ge(pad_in, 32)
                        pool.wait_ge(pool_set, 3)
                    pool.wait_ge(mask_ready, b + 1)
                    link(nc.gpsimd.tensor_tensor(acc[:, b + 1, :], acc[:, b, :], maskb[:, 0, :], ALU.add))
                    nc.gpsimd.tensor_tensor(acc[:, b + 1, :], acc[:, b + 1, :], maskb[:, 1, :],
                                            ALU.add).then_inc(acc_ready, 1)
                    pool.wait_ge(rows_ready, b + 1)
                    pool.wait_ge(gates_ready, b + 1)
                    pool.wait_ge(slot_ready, b + 1)
                    for i in range(2):
                        for k in range(2):
                            nc.gpsimd.indirect_dma_start(
                                slots, bass.IndirectOffsetOnAxis(slotu[:, b, k, i:i + 1], axis=0),
                                rows[k][:, 2 * b + i, :], None,
                                bounds_check=NE * CAP - 1, oob_is_err=False).then_inc(scattered, 16)
            pool.wait_ge(base_out, 16 * IMG)
            for e in range(NE):
                pool.wait_ge(eog_ready, e + 1)
                if e:
                    pool.wait_ge(added, 16 * e)
                nc.gpsimd.indirect_dma_start(
                    out, bass.IndirectOffsetOnAxis(xs[:, e, ROW - 1:ROW].bitcast(U32), axis=0),
                    eog[:, e % 2, :], None, compute_op=ALU.add).then_inc(added, 16)
                if e == 0:
                    n = extra_tiles(pool)
                if e < NT:
                    with pool.If(n > 0):
                        for k in range(2):
                            nc.gpsimd.indirect_dma_start(
                                slots, bass.IndirectOffsetOnAxis(extra_slot[:, k, e:e + 1], axis=0),
                                rows[k][:, e, :], None,
                                bounds_check=(NE + NOV) * CAP - 1, oob_is_err=False).then_inc(extra_scattered, 16)
            pool.wait_ge(added, 16 * NE)

            def extra_tile(i):
                pool.wait_ge(extra_out, i + 1)
                pool.sem_inc(extra_seen, 1)
                nc.gpsimd.indirect_dma_start(
                    out, bass.IndirectOffsetOnAxis(xs[:, 0, ROW - 1:ROW].bitcast(U32), axis=0),
                    eog[:, 0, :], None, compute_op=ALU.add).then_inc(extra_added, 16)
                pool.wait_ge(extra_added, 16 * i + 16)

            with pool.If(n > 0):
                extra_tile(0)
            later_tiles(pool, n, extra_tile)

        def bring_group(act, group):
            act.wait_ge(pv_done, 4 * group + 4)
            b = group // 3
            if b >= 2:
                computed(act, "D1", b - 2, 1)
            nc.scalar.copy(oT[:, b % 2, group % 3, :],
                           ps[:, 4 + group % 2, 0:NQ]).then_inc(oT_ready, 1)

        @block.scalar
        def _(act):
            act.dma_start(con[:, :], consts).then_inc(con_in, 16)
            act.wait_ge(pool_link, 2)
            nc.scalar.activation(warm[:, 0:1], padrow[:, 0:1], ACT.Exp)
            act.dma_start(rowb[:, 0, :], tokb.to_broadcast([TP, D])).then_inc(row_in, 16)
            act.dma_start(qkb_sb[:, :], qkb).then_inc(row_in, 16)
            act.dma_start(rowb[:, 1, :], vb.to_broadcast([TP, D])).then_inc(row_in, 16)
            act.dma_start(rowb[:, 2, :], outb.to_broadcast([TP, D])).then_inc(row_in, 16)
            act.wait_ge(pool_set, 1)
            act.dma_start(slots.rearrange("(t p) c -> p t c", p=CAP),
                          padrow[:, :].unsqueeze(1).to_broadcast([P, NE + NOV, ROW])).then_inc(pad_in, 16)
            act.dma_start(out[TOK:TOK + P, :], padrow[:, 0:D]).then_inc(pad_in, 16)

            act.wait_ge(con_in, 16)
            for b in range(IMG):
                act.wait_ge(clipped, b + 1)
                nc.scalar.activation(xq[:, :, NQ * b:NQ * (b + 1)], image(x_sb[0:KC, :], b), ACT.Identity,
                                     bias=con[0:KC, C_MAGIC:C_MAGIC + 1]).then_inc(quantised, 1)
            act.wait_ge(row_in, 64)
            for kind, b, s in order:
                if kind in ("A1", "A2q", "A2k", "D2", "E1"):
                    pb = ps[0:KC, bank_of(kind, b), 0:2 * NQ].rearrange("p (k n) -> p k n", k=2)
                    computed(act, kind, b)
                if kind == "A1":
                    if b:
                        computed(act, "A3", b - 1)
                    nc.scalar.copy(xnT[:, :, :], pb).then_inc(freed_by(kind, b), 1)
                if kind in ("A2q", "A2k"):
                    i = ("A2q", "A2k").index(kind)
                    if b:
                        act.wait_ge(parts_ready[i], b)
                        act.wait_ge(parts_stored[i], 16 * b)
                    for g in range(2):
                        bias = qkb_sb[:, 2 * i + g:2 * i + g + 1]
                        nc.scalar.activation(qk[:, i, g, :], pb[:, g, :], ACT.Identity, bias=bias)
                        last = nc.scalar.activation(parts[:, i, g, 0, :], pb[:, g, :], ACT.Identity, bias=bias)
                    last.then_inc(whole_ready[i], 1)
                    act.wait_ge(whole_ready[i], b + 1)
                    act.sem_inc(freed_by(kind, b), 1)
                if kind == "M":
                    act.wait_ge(mxp_ready, b + 1)
                    for i in range(2):
                        act.dma_start(qst[KC + i:KC + i + 1, b % 3, :, :], mxp[:, i, :]).then_inc(mxp_in, 16)
                if kind == "C":
                    n = H * b + s
                    act.wait_ge(st_done, n + 1)
                    if n >= 4:
                        act.wait_ge(pv_done, n - 3)
                    nc.scalar.activation(prob[:, n % 4, :, :],
                                         ps[0:TP, 2 + n % 2, 0:2 * NQ].rearrange("p (k n) -> p k n", k=2),
                                         ACT.Exp, scale=HD ** -0.5).then_inc(exp_done, 1)
                    for m in [n - LAG] + ([n - 1, n] if n == IMG * H - 1 else []):
                        if m >= 0 and m % 4 == 3:
                            bring_group(act, m // 4)
                if kind == "D2":
                    if b:
                        read_out(act, "D3", b - 1)
                    nc.scalar.copy(oTT[:, :, :], pb).then_inc(freed_by(kind, b), 1)
                if kind == "E1":
                    if b:
                        read_out(act, "E2", b - 1)
                    nc.scalar.copy(xn2T[:, :, :], pb).then_inc(freed_by(kind, b), 1)
                if kind == "E2":
                    read_out(act, "E2", b)
                    nc.scalar.activation(lexp[:, :, :], lg[:, :, :], ACT.Exp).then_inc(lexp_ready, 1)
                if kind == "G":
                    act.wait_ge(second_known, b + 1)
                    nc.scalar.activation(second_exp[:, :], second[:, :], ACT.Exp).then_inc(second_ready, 1)
            nc.scalar.activation(warm[:, 1:2], padrow[:, 0:1], ACT.Gelu)
            for e in range(NE):
                if e == RING:
                    n = extra_tiles(act)
                act.wait_ge(ring_in[e % RING], 48 * (e // RING + 1))
                for m in range(FC):
                    act.wait_ge(w1_done, FC * e + m + 1)
                    if m == 0 and e:
                        act.wait_ge(w2_done, e)
                    nc.scalar.activation(hT[:, m, :],
                                         ps[:, (FC * e + m) % 4, 0:CAP],
                                         ACT.Gelu, bias=ring2[:, e % RING, FC * D + m:FC * D + m + 1]
                                         ).then_inc(gelu_done, 1)

            def extra_tile(i):
                for m in range(FC):
                    act.wait_ge(extra_w1, FC * i + m + 1)
                    nc.scalar.activation(hT[:, m, :], ps[:, m % 4, 0:CAP], ACT.Gelu,
                                         bias=ring2[:, 0, FC * D + m:FC * D + m + 1]).then_inc(extra_gelu, 1)

            with act.If(n > 0):
                act.wait_ge(w2_done, NE)
                extra_tile(0)
            later_tiles(act, n, extra_tile)

        @block.vector
        def _(dve):
            links = [0]

            def link(ins):
                links[0] += 1
                ins.then_inc(dve_link, 1)
                dve.wait_ge(dve_link, links[0])

            V = nc.vector
            link(V.memset(ones[:, :], 1.0))
            link(V.memset(acc[:, 0, :], 0.0))
            link(V.memset(onesb[:, :], 1.0))
            dve.wait_ge(con_in, 16)
            link(V.tensor_copy(ltb[:, :], con[0:TP, C_LT:C_LT + TP]))
            dve.wait_ge(wt_in, 16)
            V.tensor_reduce(amax[:, 1:2], wt_sb[:, :], AX, ALU.max,
                            apply_absolute_value=True).then_inc(amax_ready, 1)
            dve.wait_ge(x_in, 16)
            V.tensor_reduce(amax[:, 0:1], x_sb[0:KC, :], AX, ALU.max,
                            apply_absolute_value=True).then_inc(amax_ready, 1)
            dve.wait_ge(amax_turned, 1)
            link(V.tensor_reduce(qs[:, 0:1], ps[0:2, 5, 0:KC], AX, ALU.max))
            link(V.tensor_scalar(qs[:, 1:2], qs[:, 0:1], 1e-8, 1.0 / 127.0, ALU.max, ALU.mult))
            V.tensor_scalar(qs[:, 2:4], con[0:2, C_ID:C_ID + 2], qs[:, 1:2], None, ALU.mult).then_inc(scale_diag, 1)
            dve.wait_ge(scale_spread, 1)
            link(V.tensor_copy(sc[:, 0:2], ps[:, 5, 256:258]))
            link(V.tensor_tensor(sc[:, 2:3], sc[:, 0:1], sc[:, 1:2], ALU.mult))
            V.reciprocal(sc[:, 3:5], sc[:, 0:2]).then_inc(scales_ready, 1)
            dve.wait_ge(scales_ready, 1)
            halves = wt_sb[:, :].rearrange("p (k n) -> p k n", k=2)
            V.tensor_scalar(halves, halves, sc[0:KC, 4:5], 127.0, ALU.mult, ALU.min).then_inc(dve_link, 1)
            links[0] += 1
            for b in range(IMG):
                V.tensor_scalar(image(x_sb[0:KC, :], b), image(x_sb[0:KC, :], b), sc[0:KC, 3:4], 127.0,
                                ALU.mult, ALU.min).then_inc(dve_link, 1)
                links[0] += 1
                if b == 0:
                    dve.wait_ge(dve_link, links[0] - 1)
                    link(V.tensor_scalar(halves, halves, -127.0, MAGIC, ALU.max, ALU.add))
                    V.tensor_scalar(wtq[:, :, :], halves, MAGIC, None, ALU.subtract).then_inc(weights_quantised, 1)
                else:
                    dve.wait_ge(dve_link, links[0])
                V.tensor_scalar(image(x_sb[0:KC, :], b), image(x_sb[0:KC, :], b), -127.0, MAGIC,
                                ALU.max, ALU.add).then_inc(clipped, 1)

            def embed(b):
                dve.wait_ge(tok_done, b + 1)
                V.scalar_tensor_tensor(h[:, 2 * b:2 * b + 2, :],
                                       ps[0:TP, b, 0:2 * D].rearrange("p (t d) -> p t d", t=2), sc[0:TP, 2:3],
                                       rowb[:, 0, :].unsqueeze(1).to_broadcast([TP, 2, D]),
                                       ALU.mult, ALU.add).then_inc(h_ready, 1)

            def moments(tiles, link_last):
                for t in tiles:
                    last = V.bn_stats(stats[:, t, :], h[:, t, :])
                link(last)
                for t in tiles:
                    last = V.bn_aggr(mv[:, t, :], stats[:, t, :])
                link_last(last)

            def inverse_root(tiles):
                var, y, t = first_guess(V, tiles, link)
                for _ in range(3):
                    link(V.tensor_tensor(t, y, y, ALU.mult))
                    link(V.scalar_tensor_tensor(t, t, -0.5, var, ALU.mult, ALU.mult))
                    link(V.scalar_tensor_tensor(y, t, 1.5, y, ALU.add, ALU.mult))

            def normalise(tiles, dst, done):
                for t in tiles:
                    V.tensor_scalar(dst[:, t, 0:D], h[:, t, :], mv[:, t, 0:1], rstd[:, t:t + 1],
                                    ALU.subtract, ALU.mult).then_inc(done, 1)

            def layernorm(tiles, dst, done):
                moments(tiles, link)
                inverse_root(tiles)
                normalise(tiles, dst, done)

            def over_experts(ap):
                return ap.unsqueeze(2).to_broadcast([TP, 2, NE])

            def constant(c):
                return con[0:TP, c:c + NE].unsqueeze(1).to_broadcast([TP, 2, NE])

            def choose(b):
                t2 = slice(2 * b, 2 * b + 2)
                logits = ps[0:TP, bank_of("E2", b), 0:2 * NE].rearrange("p (t e) -> p t e", t=2)
                link(V.tensor_reduce(top[:, :], logits, AX, ALU.max))
                V.tensor_tensor(lg[:, :, :], logits, over_experts(top[:, :]),
                                ALU.subtract).then_inc(freed_by("E2", b), 1)
                read_out(dve, "E2", b)
                link(V.scalar_tensor_tensor(top_sel[:, :, :], lg[:, :, :], 0.0, constant(C_REV),
                                            ALU.is_ge, ALU.mult))
                link(V.tensor_reduce(top_mark[:, :], top_sel[:, :, :], AX, ALU.max))
                link(V.tensor_tensor(oh[:, 0, t2, :], top_sel[:, :, :], over_experts(top_mark[:, :]), ALU.is_equal))
                link(V.scalar_tensor_tensor(others[:, :, :], oh[:, 0, t2, :], -LARGE, lg[:, :, :],
                                            ALU.mult, ALU.add))
                V.tensor_reduce(second[:, :], others[:, :, :], AX, ALU.max).then_inc(second_known, 1)
                dve.wait_ge(second_known, b + 1)
                link(V.tensor_tensor(second_sel[:, :, :], others[:, :, :], over_experts(second[:, :]), ALU.is_ge))
                link(V.tensor_tensor(second_sel[:, :, :], second_sel[:, :, :], constant(C_REV), ALU.mult))
                link(V.tensor_reduce(second_mark[:, :], second_sel[:, :, :], AX, ALU.max))
                link(V.tensor_tensor(oh[:, 1, t2, :], second_sel[:, :, :], over_experts(second_mark[:, :]),
                                     ALU.is_equal))
                if b:
                    dve.wait_ge(acc_ready, b)
                V.tensor_tensor(maskb[:, :, :], oh[:, 0, t2, :], oh[:, 1, t2, :], ALU.add).then_inc(mask_ready, 1)
                dve.wait_ge(lexp_ready, b + 1)
                link(V.tensor_reduce(lsum[:, :], lexp[:, :, :], AX, ALU.add))
                link(V.reciprocal(rows[0][:, t2, D:D + 1], lsum[:, :].unsqueeze(2)))
                dve.wait_ge(second_ready, b + 1)
                V.tensor_tensor(rows[1][:, t2, D:D + 1], rows[0][:, t2, D:D + 1], second_exp[:, :].unsqueeze(2),
                                ALU.mult).then_inc(gates_ready, 1)

            def place(b):
                t2 = slice(2 * b, 2 * b + 2)
                ranks = ps[0:TP, bank_of("E3", b), 0:2 * NE].rearrange("p (t e) -> p t e", t=2)
                link(V.tensor_scalar(big[:, :, :], ranks, float(CAP), BIG, ALU.is_ge, ALU.mult))
                V.tensor_tensor(rkv[:, t2, :], ranks, constant(C_E128), ALU.add).then_inc(freed_by("E3", b), 1)
                read_out(dve, "E3", b)
                link(V.tensor_tensor(big[:, :, :], big[:, :, :], rkv[:, t2, :], ALU.add))
                for k in range(2):
                    last = V.tensor_tensor(sel[:, k, :, :], oh[:, k, t2, :], big[:, :, :], ALU.mult)
                link(last)
                link(V.tensor_reduce(slotf[:, b, :, :], sel[:, :, :, :], AX, ALU.add))
                V.tensor_copy(slotu[:, b, :, :], slotf[:, b, :, :]).then_inc(slot_ready, 1)

            dve.wait_ge(row_in, 64)
            embed(0)
            dve.wait_ge(h_ready, 1)
            layernorm(range(2), xn1, xn1_ready)
            for b in range(1, IMG):
                embed(b)
            dve.wait_ge(h_ready, IMG)
            layernorm(range(2, 4), xn1, xn1_ready)
            dve.wait_ge(whole_ready[1], 1)
            split(V, 1, link)
            for kind, b, i in order:
                if kind == "A3":
                    computed(dve, kind, b)
                    if b == 0:
                        dve.wait_ge(pool_set, 4)
                    if b >= 3:
                        dve.wait_ge(pv_done, H * (b - 2))
                    V.tensor_tensor(vaug[:, b % 3, :, :, 0:HD],
                                    ps[0:TP, bank_of(kind, b), 0:2 * D].rearrange("p (t h d) -> p t h d", t=2, h=H),
                                    rowb[:, 1, :].rearrange("p (h d) -> p h d", h=H).unsqueeze(1)
                                    .to_broadcast([TP, 2, H, HD]), ALU.add).then_inc(freed_by(kind, b), 1)
                    if b == 0:
                        layernorm(range(4, NT), xn1, xn1_ready)
                if kind == "B":
                    n = H * b + i
                    dve.wait_ge(s_done, n + 1)
                    if i == 0 and b:
                        read_out(dve, "N", b - 1)
                    V.tensor_reduce(mx[:, i // 6, 2 * (i % 6):2 * (i % 6) + 2],
                                    ps[0:TP, n % 2, 0:2 * NQ].rearrange("p (h n) -> p h n", h=2),
                                    AX, ALU.max).then_inc(mx_ready, 1)
                if kind == "N":
                    computed(dve, kind, b)
                    if b:
                        dve.wait_ge(mxp_in, 32 * b)
                    maxima = ps[0:H, bank_of(kind, b), 0:NQ]
                    link(V.tensor_scalar(mxp[:, 0, :], maxima, -1.0, None, ALU.mult))
                    V.scalar_tensor_tensor(mxp[:, 1, :], maxima, -1.0, mxp[:, 0, :], ALU.mult,
                                           ALU.subtract).then_inc(freed_by(kind, b), 1)
                    read_out(dve, kind, b)
                    dve.sem_inc(mxp_ready, 1)
                if kind == "D1":
                    if b:
                        read_out(dve, "D2", b - 1)
                    for j in range(2):
                        computed(dve, kind, b, j)
                        heads = ps[0:TP, bank_of(kind, b, j), 0:3 * P].rearrange("p (h d) -> p h d", d=32)
                        link(V.reciprocal(rec[:, j, :], heads[:, :, HD]))
                        V.tensor_tensor(otok[:, j, :].rearrange("p (h d) -> p h d", h=H), heads[:, :, 0:HD],
                                        rec[:, j, :].unsqueeze(2).to_broadcast([TP, H, HD]),
                                        ALU.mult).then_inc(freed_by(kind, b, j), 1)
                if kind == "D3":
                    computed(dve, kind, b)
                    dve.wait_ge(hb_ready, b + 1)
                    V.tensor_tensor(h[:, 2 * b:2 * b + 2, :],
                                    ps[0:TP, bank_of(kind, b), 0:2 * D].rearrange("p (t d) -> p t d", t=2),
                                    h[:, 2 * b:2 * b + 2, :], ALU.add).then_inc(freed_by(kind, b), 1)
                    read_out(dve, kind, b)
                    if b < IMG - 2:
                        moments(range(2 * b, 2 * b + 2), lambda last: last.then_inc(moments_ready, 1))
                    else:
                        moments(range(2 * b, 2 * b + 2), link)
                        inverse_root(range(2 * b, 2 * b + 2))
                        dve.sem_inc(rstd_ready, 1)
                if kind == "L":
                    dve.wait_ge(rstd_ready, b + 1)
                    normalise(range(2 * b, 2 * b + 2), rows[0], xn2_ready)
                if kind == "E2":
                    computed(dve, kind, b)
                    choose(b)
                if kind == "E3":
                    computed(dve, kind, b)
                    place(b)

            def bring_tokens(e):
                dve.wait_ge(t_done, e + 1)
                if e >= 2:
                    dve.wait_ge(w1_done, FC * (e - 1))
                V.tensor_copy(xsT[:, e % 2, :, :],
                              ps[0:KC, 6 + e % 2, 0:2 * CAP].rearrange("p (k n) -> p k n", k=2)
                              ).then_inc(xsT_ready, 1)

            dve.wait_ge(counted, 1)
            cmp6 = extra_cmp[:, 0:NE * 6].rearrange("p (e j) -> p e j", j=6)
            V.tensor_tensor(cmp6, ps[0:TP, 5, 0:NE].unsqueeze(2).to_broadcast([TP, NE, 6]),
                                con[0:TP, C_THR:C_THR + 6].unsqueeze(1).to_broadcast([TP, NE, 6]),
                                ALU.is_gt).then_inc(counts_read, 1)

            def find_extra():
                of, upto, start = (extra_e[:, i, :] for i in range(3))
                dve.wait_ge(counts_read, 1)
                link(V.tensor_reduce(of, cmp6, AX, ALU.add))
                square = extra_cmp.rearrange("p (e f) -> p e f", e=NE)
                link(V.tensor_tensor(square, of.unsqueeze(1).to_broadcast([TP, NE, NE]),
                                     con[0:TP, C_TRI16:C_TRI16 + NE * NE].rearrange("p (e f) -> p e f", e=NE),
                                     ALU.mult))
                link(V.tensor_reduce(upto, square, AX, ALU.add))
                link(V.tensor_tensor(start, upto, of, ALU.subtract))
                link(V.scalar_tensor_tensor(start, start, float(CAP), con[0:TP, C_OVC:C_OVC + NE],
                                            ALU.mult, ALU.add))

                def all_tiles(ap):
                    return ap.unsqueeze(1).to_broadcast([TP, NT, NE])

                val, small = extra_val[:, 0, :, :], extra_val[:, 1, :, :]
                link(V.tensor_tensor(small, rkv[:, :, :], all_tiles(con[0:TP, C_E128:C_E128 + NE]), ALU.subtract))
                link(V.tensor_scalar(small, small, float(CAP), BIG, ALU.is_lt, ALU.mult))
                link(V.tensor_tensor(val, rkv[:, :, :], all_tiles(start), ALU.add))
                link(V.tensor_tensor(val, val, small, ALU.add))
                for k in range(2):
                    last = V.tensor_tensor(extra_sel[:, k, :, :], oh[:, k, :, :], val, ALU.mult)
                link(last)
                link(V.tensor_reduce(extra_slotf, extra_sel, AX, ALU.add))
                link(V.tensor_copy(extra_slot, extra_slotf))
                table = extra_cmp[0:1, 0:NOV * NE].rearrange("p (i e) -> p i e", i=NOV)
                link(V.tensor_tensor(table, upto[0:1, :].unsqueeze(1).to_broadcast([1, NOV, NE]),
                                     con[0:1, C_I12:C_I12 + NOV].unsqueeze(2).to_broadcast([1, NOV, NE]),
                                     ALU.is_le))
                link(V.tensor_reduce(extra_idf[:, 0:NOV], table, AX, ALU.add))
                link(V.tensor_scalar(extra_idf[:, 0:NOV], extra_idf[:, 0:NOV], float(NE - 1), None, ALU.min))
                link(V.tensor_copy(extra_idf[:, NOV:NOV + 1], upto[0:1, NE - 1:NE]))
                V.tensor_copy(extra_id, extra_idf).then_inc(extra_known, 1)

            def bring_extra(i):
                dve.wait_ge(extra_turned, i + 1)
                V.tensor_copy(xsT[:, 0, :, :],
                              ps[0:KC, 6, 0:2 * CAP].rearrange("p (k n) -> p k n", k=2)).then_inc(extra_x, 1)

            bring_tokens(0)
            for e in range(NE):
                if e + 1 < NE:
                    bring_tokens(e + 1)
                else:
                    with dve.If(n > 0):
                        bring_extra(0)
                if e == 0:
                    find_extra()
                if e == RING:
                    n = extra_tiles(dve)
                dve.wait_ge(w2_done, e + 1)
                dve.wait_ge(ring_in[e % RING], 48 * (e // RING + 1))
                V.tensor_tensor(eo[:, e % 2, :], ps[:, 4 + e % 2, 0:D], ringb[:, e % RING, :],
                                ALU.add).then_inc(eo_ready, 1)
                dve.wait_ge(eo_ready, e + 1)
                dve.wait_ge(xs_in[load_of(e)], 16)
                if e >= 2:
                    dve.wait_ge(added, 16 * (e - 1))
                V.tensor_scalar(eog[:, e % 2, :], eo[:, e % 2, :], xs[:, e, D:D + 1], None,
                                ALU.mult).then_inc(eog_ready, 1)

            def extra_tile(i):
                dve.wait_ge(extra_w2, i + 1)
                V.tensor_tensor(eo[:, 0, :], ps[:, 4, 0:D], ringb[:, 0, :], ALU.add).then_inc(extra_sum, 1)
                dve.wait_ge(extra_sum, i + 1)
                V.tensor_scalar(eog[:, 0, :], eo[:, 0, :], xs[:, 0, D:D + 1], None,
                                ALU.mult).then_inc(extra_out, 1)

            with dve.If(n > 0):
                dve.wait_ge(added, 16 * (NE - 1))
                extra_tile(0)

            def later_tile(i):
                bring_extra(i)
                extra_tile(i)

            later_tiles(dve, n, later_tile)

        @block.tensor
        def _(pe):
            mm, tr = nc.tensor.matmul, nc.tensor.transpose

            def stay_awake(count, bank=5):
                for _ in range(count):
                    mm(ps[:, bank, :], wtq[:, 0, 0:P], xq[:, 0, 0:512], start=True, stop=True)

            def warm_up(columns):
                mm(ps[:, 7, 0:columns], ones[:, :], con[:, 0:columns], start=True, stop=True)

            pe.wait_ge(con_in, 16)
            pe.wait_ge(amax_ready, 2)
            tr(ps[0:2, 5, 0:KC], amax[:, :], ident[0:KC, 0:KC]).then_inc(amax_turned, 1)
            pe.wait_ge(scale_diag, 1)
            mm(ps[:, 5, 256:258], ones[0:2, :], qs[:, 2:4], start=True, stop=True).then_inc(scale_spread, 1)
            for _ in range(WARM_SCALES):
                warm_up(4 * P)
            pe.wait_ge(weights_quantised, 1)
            for t in range(NT):
                if t % 2 == 0:
                    if t:
                        warm_up(P)
                    pe.wait_ge(quantised, t // 2 + 1)
                for k in range(2):
                    last = mm(ps[0:TP, t // 2, D * (t % 2):D * (t % 2 + 1)], xq[:, k, TP * t:TP * (t + 1)],
                              wtq[:, k, :], start=(k == 0), stop=(k == 1))
                if t % 2:
                    last.then_inc(tok_done, 1)
            stay_awake(AWAKE_TOKENS)
            pe.wait_ge(small_in, 48)

            def values(n):
                b, hd = n // H, n % H
                pe.wait_ge(exp_done, n + 1)
                if hd == 0:
                    read_out(pe, "A3", b)
                if n == 0:
                    pe.wait_ge(pool_set, 4)
                group = n // 4
                if group >= 2 and n % 4 == 0:
                    pe.wait_ge(oT_ready, group - 1)
                for kt in range(2):
                    last = mm(ps[32 * (n % 4):32 * (n % 4) + 32, 4 + group % 2, 0:NQ],
                              vaug[:, b % 3, kt, hd, :], prob[:, n % 4, kt, :], start=(kt == 0), stop=(kt == 1),
                              skip_group_check=True)
                last.then_inc(pv_done, 1)

            for kind, b, s in order:
                if kind in ("A1", "A2q", "A2k", "A3", "N", "D2", "D3", "E1", "E2", "E3"):
                    bank_is_free(pe, kind, b)
                    bank = bank_of(kind, b)
                if kind == "A1":
                    pe.wait_ge(xn1_ready, 2 * (b + 1))
                    for k in range(2):
                        for t in range(2):
                            last = tr(ps[0:KC, bank, NQ * k + TP * t:NQ * k + TP * (t + 1)],
                                      xn1[:, 2 * b + t, KC * k:KC * (k + 1)], ident[0:TP, 0:TP])
                    last.then_inc(misc_ready, 1)
                if kind in ("A2q", "A2k"):
                    if kind == "A2q":
                        read_out(pe, "A1", b)
                    at = 0 if kind == "A2q" else D
                    for g in range(2):
                        for k in range(2):
                            last = mm(ps[0:KC, bank, NQ * g:NQ * (g + 1)],
                                      wqkv_sb[:, k, at + KC * g:at + KC * (g + 1)], xnT[:, k, :],
                                      start=(k == 0), stop=(k == 1))
                    last.then_inc(misc_ready, 1)
                if kind == "A3":
                    for t in range(2):
                        for k in range(2):
                            last = mm(ps[0:TP, bank, D * t:D * (t + 1)], xnT[:, k, TP * t:TP * (t + 1)],
                                      wqkv_sb[:, k, 2 * D:3 * D], start=(k == 0), stop=(k == 1))
                    last.then_inc(misc_ready, 1)
                if kind == "B":
                    n = H * b + s
                    if s == 0:
                        pe.wait_ge(stack_in[0], 16 * len(STACK[0]) * (b + 1))
                        pe.wait_ge(stack_in[1], 16 * len(STACK[1]) * (b + 1))
                    if n == 0:
                        pe.wait_ge(h_ready, IMG)
                    if n >= 2:
                        pe.wait_ge(mx_ready, n - 1)
                    stay_awake(AWAKE_MAXIMA[b], n % 2)
                    qt = s // 6
                    for j in range(2):
                        hd = 2 * (s % 6) + j
                        last = mm(ps[0:TP, n % 2, NQ * j:NQ * (j + 1)], qst[0:KC, b % 3, hd, TP * qt:TP * (qt + 1)],
                                  kst[0:KC, b % 3, hd, :], start=True, stop=True)
                    last.then_inc(s_done, 1)
                if kind == "N":
                    pe.wait_ge(mx_ready, H * (b + 1))
                    for t in range(2):
                        last = tr(ps[0:H, bank, TP * t:TP * (t + 1)], mx[:, t, :], ident[0:TP, 0:TP])
                    last.then_inc(misc_ready, 1)
                if kind == "C":
                    n = H * b + s
                    if s == 0:
                        pe.wait_ge(mxp_in, 32 * (b + 1))
                    if n == 0:
                        pe.wait_ge(pool_set, 5)
                    if n >= 2:
                        pe.wait_ge(exp_done, n - 1)
                    stay_awake(AWAKE_LAST_SCORES if n >= IMG * H - 3 else AWAKE_SCORES, 2 + n % 2)
                    for kt in range(2):
                        last = mm(ps[0:TP, 2 + n % 2, NQ * kt:NQ * (kt + 1)],
                                  kst[:, b % 3, s, TP * kt:TP * (kt + 1)], qst[:, b % 3, s, :],
                                  start=True, stop=True)
                    last.then_inc(st_done, 1)
                    if n >= LAG:
                        values(n - LAG)
                    if n == IMG * H - 1:
                        values(n - 1)
                        values(n)
                if kind == "D1":
                    pe.wait_ge(oT_ready, 3 * (b + 1))
                    for t in range(2):
                        bank_is_free(pe, kind, b, t)
                        for r in range(3):
                            last = tr(ps[0:TP, bank_of(kind, b, t), P * r:P * (r + 1)],
                                      oT[:, b % 2, r, TP * t:TP * (t + 1)], ident)
                        last.then_inc(misc_ready, 1)
                if kind == "D2":
                    read_out(pe, "D1", b, 0)
                    read_out(pe, "D1", b, 1)
                    for k in range(2):
                        for t in range(2):
                            last = tr(ps[0:KC, bank, NQ * k + TP * t:NQ * k + TP * (t + 1)],
                                      otok[:, t, KC * k:KC * (k + 1)], ident[0:TP, 0:TP])
                    last.then_inc(misc_ready, 1)
                if kind == "D3":
                    read_out(pe, "D2", b)
                    for t in range(2):
                        for k in range(2):
                            last = mm(ps[0:TP, bank, D * t:D * (t + 1)], oTT[:, k, TP * t:TP * (t + 1)],
                                      wo_sb[:, k, :], start=(k == 0), stop=(k == 1))
                    last.then_inc(misc_ready, 1)
                if kind == "E1":
                    pe.wait_ge(xn2_ready, 2 * (b + 1))
                    for k in range(2):
                        for t in range(2):
                            last = tr(ps[0:KC, bank, NQ * k + TP * t:NQ * k + TP * (t + 1)],
                                      rows[0][:, 2 * b + t, KC * k:KC * (k + 1)], ident[0:TP, 0:TP])
                    last.then_inc(misc_ready, 1)
                if kind == "E2":
                    read_out(pe, "E1", b)
                    for t in range(2):
                        for k in range(2):
                            last = mm(ps[0:TP, bank, NE * t:NE * (t + 1)], xn2T[:, k, TP * t:TP * (t + 1)],
                                      wr_sb[:, k, :], start=(k == 0), stop=(k == 1))
                    last.then_inc(misc_ready, 1)
                stay_awake(AWAKE.get((kind, b), 0))
                if kind == "E3":
                    pe.wait_ge(mask_ready, b + 1)
                    if b:
                        pe.wait_ge(acc_ready, b)
                    mm(ps[0:TP, bank, 0:NE], ltb[:, :], maskb[:, 0, :], start=True, stop=False)
                    mm(ps[0:TP, bank, 0:NE], onesb[:, :], acc[:, b, :], start=False, stop=True)
                    mm(ps[0:TP, bank, NE:2 * NE], ltb[:, :], maskb[:, 1, :], start=True, stop=False)
                    mm(ps[0:TP, bank, NE:2 * NE], onesb[:, :], maskb[:, 0, :], start=False, stop=False)
                    mm(ps[0:TP, bank, NE:2 * NE], onesb[:, :], acc[:, b, :], start=False,
                       stop=True).then_inc(misc_ready, 1)

            pe.wait_ge(acc_ready, IMG)
            mm(ps[0:TP, 5, 0:NE], onesb[:, :], acc[:, IMG, :], start=True, stop=True).then_inc(counted, 1)

            pe.wait_ge(counts_read, 1)
            stay_awake(AWAKE_COUNTS)

            def turn_tokens(e):
                pe.wait_ge(xs_in[load_of(e)], 16)
                if e >= 2:
                    pe.wait_ge(xsT_ready, e - 1)
                for k in range(2):
                    last = tr(ps[0:KC, 6 + e % 2, CAP * k:CAP * (k + 1)], xs[:, e, KC * k:KC * (k + 1)], ident)
                last.then_inc(t_done, 1)

            def turn_extra(i):
                pe.wait_ge(extra_in, 64 * i + 64)
                for k in range(2):
                    last = tr(ps[0:KC, 6, CAP * k:CAP * (k + 1)], xs[:, 0, KC * k:KC * (k + 1)], ident)
                last.then_inc(extra_turned, 1)

            turn_tokens(0)
            for e in range(NE):
                r = e % RING
                if e == RING:
                    n = extra_tiles(pe)
                pe.wait_ge(ring_in[r], 48 * (e // RING + 1))
                pe.wait_ge(xsT_ready, e + 1)
                for m in range(FC):
                    if FC * e + m >= 4:
                        pe.wait_ge(gelu_done, FC * e + m - 3)
                    for k in range(2):
                        last = mm(ps[:, (FC * e + m) % 4, 0:CAP],
                                  ring1[:, r, FF * k + P * m:FF * k + P * (m + 1)], xsT[:, e % 2, k, :],
                                  start=(k == 0), stop=(k == 1))
                    last.then_inc(w1_done, 1)
                if e + 1 < NE:
                    turn_tokens(e + 1)
                else:
                    with pe.If(n > 0):
                        turn_extra(0)
                if e >= 2:
                    pe.wait_ge(eo_ready, e - 1)
                for m in range(FC):
                    pe.wait_ge(gelu_done, FC * e + m + 1)
                    last = mm(ps[:, 4 + e % 2, 0:D], hT[:, m, :], ring2[:, r, D * m:D * (m + 1)],
                              start=(m == 0), stop=(m == FC - 1))
                last.then_inc(w2_done, 1)

            def extra_tile(i):
                pe.wait_ge(extra_x, i + 1)
                for m in range(FC):
                    if m >= 4:
                        pe.wait_ge(extra_gelu, FC * i + m - 3)
                    for k in range(2):
                        last = mm(ps[:, m % 4, 0:CAP], ring1[:, 0, FF * k + P * m:FF * k + P * (m + 1)],
                                  xsT[:, 0, k, :], start=(k == 0), stop=(k == 1))
                    last.then_inc(extra_w1, 1)
                for m in range(FC):
                    pe.wait_ge(extra_gelu, FC * i + m + 1)
                    last = mm(ps[:, 4, 0:D], hT[:, m, :], ring2[:, 0, D * m:D * (m + 1)],
                              start=(m == 0), stop=(m == FC - 1))
                last.then_inc(extra_w2, 1)

            with pe.If(n > 0):
                pe.wait_ge(gelu_done, FC * NE)
                pe.wait_ge(eo_ready, NE - 1)
                extra_tile(0)

            def later_tile(i):
                turn_extra(i)
                extra_tile(i)

            later_tiles(pe, n, later_tile)


def constants():
    import numpy as np
    c = np.zeros((P, C_N), np.float32)
    p = np.arange(P)
    c[:, C_ID:C_ID + P] = np.eye(P)
    c[:, C_MAGIC] = -MAGIC
    e = np.arange(NE)
    c[:, C_REV:C_REV + NE] = NE - e
    c[:, C_E128:C_E128 + NE] = CAP * e
    c[:, C_THR:C_THR + 6] = CAP * np.arange(1, 7)
    c[:, C_TRI16:C_TRI16 + NE * NE] = (e[None, :] <= e[:, None]).reshape(-1)
    c[:, C_OVC:C_OVC + NE] = (NE - 1) * CAP - CAP * e
    c[:, C_I12:C_I12 + NOV] = np.arange(NOV)
    c[:, C_LT:C_LT + TP] = p[:, None] < np.arange(TP)[None, :]
    return c


def kernel(**inputs):
    import numpy as np
    import concourse.bacc as bacc
    from concourse import mybir as mb
    from concourse.bass_utils import run_bass_kernel_spmd as run

    a = {k: np.asarray(v) for k, v in inputs.items()}
    def chunks(m):
        return m.reshape(2, KC, m.shape[1]).transpose(1, 0, 2)

    x = a["x"].reshape(IMG, 3, 14, 8, 14, 8).transpose(1, 3, 5, 0, 2, 4).reshape(D, TOK)
    w1 = a["L0_ffn_W1"].reshape(NE, 2, KC, FF).transpose(0, 2, 1, 3).reshape(NE, KC, 2 * FF)
    w2 = a["L0_ffn_W2"].reshape(NE, FC, P, D).transpose(0, 2, 1, 3).reshape(NE, P, FC * D)
    b1 = a["L0_ffn_b1"].reshape(NE, FC, P).transpose(0, 2, 1)
    order = np.arange(3 * D)
    order[:2 * D] = order[:2 * D].reshape(4, G6, HD).transpose(0, 2, 1).reshape(-1)
    qkv_w, qkv_b = a["L0_attn_qkv_w"][order], a["L0_attn_qkv_b"][order]
    data = {
        "xp": chunks(x).reshape(KC, 2 * TOK),
        "wtok": chunks(a["L0_tok_w"].reshape(D, D).T).reshape(KC, 2 * D),
        "tokb": a["L0_tok_b"].reshape(1, D),
        "wqkv": chunks(qkv_w.T),
        "qkb": qkv_b[:2 * D].reshape(4, KC).T,
        "vb": qkv_b[2 * D:].reshape(1, D),
        "wout": chunks(a["L0_attn_out_w"].T),
        "outb": a["L0_attn_out_b"].reshape(1, D),
        "wr": chunks(a["L0_ffn_Wr"].T),
        "w1": w1,
        "w2": np.concatenate([w2, b1], axis=2),
        "b2": a["L0_ffn_b2"],
        "consts": constants(),
    }
    nc = bacc.Bacc("TRN2", target_bir_lowering=False, num_devices=1)
    arrays, args = {}, []
    for name, v in data.items():
        v = np.ascontiguousarray(v)
        arrays[name] = v
        args.append(nc.dram_tensor(name, v.shape, mb.dt.from_np(v.dtype), kind="ExternalInput").ap())
    args.append(nc.dram_tensor("out", (TOK + P, D), mb.dt.float32, kind="ExternalOutput").ap())
    vit_block(nc, *args)
    r = run(nc, [arrays], core_ids=[0])
    return r.results[0]["out"][:TOK].reshape(IMG, NQ, D)
```
